# Optimizing a Trainium2 kernel written in Bass

```python
import numpy as np
import jax
import jax.numpy as jnp

def _softmax(x, axis=-1):
    return jax.nn.softmax(x, axis=axis)

def _gelu(x):
    return jax.nn.gelu(x, approximate=True)

def _silu(x):
    return jax.nn.silu(x)

def _sigmoid(x):
    return jax.nn.sigmoid(x)

def _layernorm(x, axis=-1, eps=1e-05):
    m = jnp.mean(x, axis=axis, keepdims=True)
    v = jnp.var(x, axis=axis, keepdims=True)
    return (x - m) / jnp.sqrt(v + eps)

def _scatter_add(tgt, idx, src, axis=0):
    return tgt.at[idx].add(src)

def _segment_sum(src, seg, n):
    return jax.ops.segment_sum(src, seg, n)
kernel_name = 'mk_xattn_ffn_d2_seqx_r4_1a0239'

def setup_inputs(seed: int=0):
    np.random.seed(seed)
    _w = jnp.asarray

    def _rec_inputs():
        import jax
        import jax.numpy as jnp
        _rk = jax.random.key(seed)
        x = 7.22e-05 + 1 * jax.random.normal(jax.random.fold_in(_rk, 1), (8, 512, 256), jnp.float32)
        _lenS = 512 - jax.random.randint(jax.random.fold_in(_rk, 7), (8,), 0, max(1, 512 // 4) + 1, jnp.int32)
        _lenS2 = 512 - jax.random.randint(jax.random.fold_in(_rk, 8), (8,), 0, max(1, 512 // 4) + 1, jnp.int32)
        _ctx_1024P = jax.random.normal(jax.random.fold_in(_rk, 11), (8, 16, 256), jnp.float32)
        _ctx_1024c = jax.random.dirichlet(jax.random.fold_in(_rk, 511), 0.3 * jnp.ones((16,), jnp.float32), (8, 512))
        _ctx_1024t = jnp.einsum('bsk,bkd->bsd', _ctx_1024c, _ctx_1024P)
        _ctx_1024t = _ctx_1024t * jax.lax.rsqrt(jnp.mean(jnp.square(_ctx_1024t)) + 1e-12) * 0.953939
        ctx_1024 = 4.13588e-05 + 0.999923 * (_ctx_1024t + 0.3 * jax.random.normal(jax.random.fold_in(_rk, 611), (8, 512, 256), jnp.float32))
        _validS = jnp.arange(512)[None, :] < _lenS[:, None]
        _validS2 = jnp.arange(512)[None, :] < _lenS2[:, None]
        _causal = jnp.tril(jnp.ones((512, 512), dtype=bool))
        mask_1x1xSxS2_if1 = jnp.where(jnp.ones((1, 1, 512, 512), dtype=bool), 1, 0).astype(jnp.int32)
        return (x, ctx_1024, mask_1x1xSxS2_if1)
    x, ctx_1024, mask_1x1xSxS2_if1 = _rec_inputs()

    def _L0_xattn_setup():
        import jax, jax.numpy as jnp
        import numpy as np
        D_MODEL = 256
        N_HEAD = 16
        D_K = D_MODEL // N_HEAD
        NEG = -1000000000.0
        key = jax.random.key(seed)
        ks = jax.random.split(key, 12)
        B, S = (4, 512)
        scale = 1.0 / np.sqrt(D_MODEL)
        inp = {'q': jax.random.normal(ks[0], (B, S, D_MODEL), jnp.float32), 'k': jax.random.normal(ks[1], (B, S, D_MODEL), jnp.float32), 'v': jax.random.normal(ks[2], (B, S, D_MODEL), jnp.float32), 'mask': jnp.ones((1, 1, S, S), jnp.int32), 'w_Q': jax.random.normal(ks[3], (D_MODEL, D_MODEL), jnp.float32) * scale, 'b_Q': jnp.zeros((D_MODEL,), jnp.float32), 'w_K': jax.random.normal(ks[4], (D_MODEL, D_MODEL), jnp.float32) * scale, 'b_K': jnp.zeros((D_MODEL,), jnp.float32), 'w_V': jax.random.normal(ks[5], (D_MODEL, D_MODEL), jnp.float32) * scale, 'b_V': jnp.zeros((D_MODEL,), jnp.float32), 'w_O': jax.random.normal(ks[6], (D_MODEL, D_MODEL), jnp.float32) * scale, 'b_O': jnp.zeros((D_MODEL,), jnp.float32)}
        return inp
    _L0_xattn_all = _L0_xattn_setup()
    _L0_xattn_in = {k: v for k, v in _L0_xattn_all.items() if k in ('w_Q', 'b_Q', 'w_K', 'b_K', 'w_V', 'b_V', 'w_O', 'b_O')}
    del _L0_xattn_all

    def _L0_ffn_setup():
        import jax, jax.numpy as jnp
        import numpy as np
        IN_F, OUT_F, BLOCK, NBLK = (256, 1024, 64, 16)
        TOPK = NBLK // 4
        key = jax.random.key(seed)
        ks = jax.random.split(key, 7)
        s = 1.0 / np.sqrt(IN_F)
        s2 = 1.0 / np.sqrt(OUT_F)
        return {'x': jax.random.normal(ks[0], (4, 1024, IN_F), jnp.float32), 'router_w': jax.random.uniform(ks[1], (NBLK, IN_F), jnp.float32, -s, s), 'router_b': jax.random.uniform(ks[2], (NBLK,), jnp.float32, -s, s), 'w1': jax.random.uniform(ks[3], (OUT_F, IN_F), jnp.float32, -s, s), 'b1': jax.random.uniform(ks[4], (OUT_F,), jnp.float32, -s, s), 'w2': jax.random.uniform(ks[5], (IN_F, OUT_F), jnp.float32, -s2, s2), 'b2': jax.random.uniform(ks[6], (IN_F,), jnp.float32, -s2, s2)}
    _L0_ffn_all = _L0_ffn_setup()
    _L0_ffn_in = {k: v for k, v in _L0_ffn_all.items() if k in ('router_w', 'router_b', 'w1', 'b1', 'w2', 'b2')}
    del _L0_ffn_all

    def _L1_xattn_setup():
        import jax, jax.numpy as jnp
        import numpy as np
        B, T, D, H = (2, 512, 256, 16)
        DH = D // H
        key = jax.random.key(seed)
        ks = jax.random.split(key, 11)
        s = 1.0 / np.sqrt(D)
        return {'q': jax.random.normal(ks[0], (B, T, D), jnp.float32), 'k': jax.random.normal(ks[1], (B, T, D), jnp.float32), 'v': jax.random.normal(ks[2], (B, T, D), jnp.float32), 'wq_w': jax.random.normal(ks[3], (D, D), jnp.float32) * s, 'wq_b': jnp.zeros((D,), jnp.float32), 'wk_w': jax.random.normal(ks[4], (D, D), jnp.float32) * s, 'wk_b': jnp.zeros((D,), jnp.float32), 'wv_w': jax.random.normal(ks[5], (D, D), jnp.float32) * s, 'wv_b': jnp.zeros((D,), jnp.float32), 'wo_w': jax.random.normal(ks[6], (D, D), jnp.float32) * s, 'wo_b': jnp.zeros((D,), jnp.float32)}
    _L1_xattn_all = _L1_xattn_setup()
    _L1_xattn_in = {k: v for k, v in _L1_xattn_all.items() if k in ('wq_w', 'wq_b', 'wk_w', 'wk_b', 'wv_w', 'wv_b', 'wo_w', 'wo_b')}
    del _L1_xattn_all

    def _L1_ffn_setup():
        import jax, jax.numpy as jnp
        import numpy as np
        N_EMBD = 256
        N_STATE = 1024
        key = jax.random.key(seed)
        k_x, k_w1, k_b1, k_w2, k_b2 = jax.random.split(key, 5)
        x = jax.random.normal(k_x, (4, 512, N_EMBD), dtype=jnp.float32)
        w1 = jax.random.normal(k_w1, (N_EMBD, N_STATE), dtype=jnp.float32) * (1.0 / np.sqrt(N_EMBD))
        b1 = jax.random.normal(k_b1, (N_STATE,), dtype=jnp.float32) * 0.02
        w2 = jax.random.normal(k_w2, (N_STATE, N_EMBD), dtype=jnp.float32) * (1.0 / np.sqrt(N_STATE))
        b2 = jax.random.normal(k_b2, (N_EMBD,), dtype=jnp.float32) * 0.02
        return {'x': x, 'w1': w1, 'b1': b1, 'w2': w2, 'b2': b2}
    _L1_ffn_all = _L1_ffn_setup()
    _L1_ffn_in = {k: v for k, v in _L1_ffn_all.items() if k in ('w1', 'b1', 'w2', 'b2')}
    del _L1_ffn_all
    return {'x': x, 'ctx_1024': ctx_1024, 'mask_1x1xSxS2_if1': mask_1x1xSxS2_if1, 'L0_xattn_w_Q': _L0_xattn_in['w_Q'], 'L0_xattn_b_Q': _L0_xattn_in['b_Q'], 'L0_xattn_w_K': _L0_xattn_in['w_K'], 'L0_xattn_b_K': _L0_xattn_in['b_K'], 'L0_xattn_w_V': _L0_xattn_in['w_V'], 'L0_xattn_b_V': _L0_xattn_in['b_V'], 'L0_xattn_w_O': _L0_xattn_in['w_O'], 'L0_xattn_b_O': _L0_xattn_in['b_O'], 'L0_ffn_router_w': _L0_ffn_in['router_w'], 'L0_ffn_router_b': _L0_ffn_in['router_b'], 'L0_ffn_w1': _L0_ffn_in['w1'], 'L0_ffn_b1': _L0_ffn_in['b1'], 'L0_ffn_w2': _L0_ffn_in['w2'], 'L0_ffn_b2': _L0_ffn_in['b2'], 'L1_xattn_wq_w': _L1_xattn_in['wq_w'], 'L1_xattn_wq_b': _L1_xattn_in['wq_b'], 'L1_xattn_wk_w': _L1_xattn_in['wk_w'], 'L1_xattn_wk_b': _L1_xattn_in['wk_b'], 'L1_xattn_wv_w': _L1_xattn_in['wv_w'], 'L1_xattn_wv_b': _L1_xattn_in['wv_b'], 'L1_xattn_wo_w': _L1_xattn_in['wo_w'], 'L1_xattn_wo_b': _L1_xattn_in['wo_b'], 'L1_ffn_w1': _L1_ffn_in['w1'], 'L1_ffn_b1': _L1_ffn_in['b1'], 'L1_ffn_w2': _L1_ffn_in['w2'], 'L1_ffn_b2': _L1_ffn_in['b2']}

def reference(x, ctx_1024, mask_1x1xSxS2_if1, L0_xattn_w_Q, L0_xattn_b_Q, L0_xattn_w_K, L0_xattn_b_K, L0_xattn_w_V, L0_xattn_b_V, L0_xattn_w_O, L0_xattn_b_O, L0_ffn_router_w, L0_ffn_router_b, L0_ffn_w1, L0_ffn_b1, L0_ffn_w2, L0_ffn_b2, L1_xattn_wq_w, L1_xattn_wq_b, L1_xattn_wk_w, L1_xattn_wk_b, L1_xattn_wv_w, L1_xattn_wv_b, L1_xattn_wo_w, L1_xattn_wo_b, L1_ffn_w1, L1_ffn_b1, L1_ffn_w2, L1_ffn_b2):
    import jax
    import jax.numpy as jnp

    def _L0_xattn_ref(q, k, v, mask, w_Q, b_Q, w_K, b_K, w_V, b_V, w_O, b_O):
        import jax, jax.numpy as jnp
        import numpy as np
        D_MODEL = 256
        N_HEAD = 16
        D_K = D_MODEL // N_HEAD
        NEG = -1000000000.0
        B, S, _ = q.shape
        qp = q @ w_Q.T + b_Q
        kp = k @ w_K.T + b_K
        vp = v @ w_V.T + b_V
        qh = qp.reshape(B, S, N_HEAD, D_K).transpose(0, 2, 1, 3)
        kh = kp.reshape(B, S, N_HEAD, D_K).transpose(0, 2, 1, 3)
        vh = vp.reshape(B, S, N_HEAD, D_K).transpose(0, 2, 1, 3)
        scores = jnp.einsum('bhqd,bhkd->bhqk', qh, kh) / jnp.sqrt(jnp.float32(D_K))
        scores = jnp.where(mask == 0, jnp.float32(NEG), scores)
        attn = jax.nn.softmax(scores, axis=-1)
        ctx = jnp.einsum('bhqk,bhkd->bhqd', attn, vh)
        ctx = ctx.transpose(0, 2, 1, 3).reshape(B, S, D_MODEL)
        return ctx @ w_O.T + b_O

    def _L0_ffn_ref(x, router_w, router_b, w1, b1, w2, b2):
        import jax, jax.numpy as jnp
        import numpy as np
        IN_F, OUT_F, BLOCK, NBLK = (256, 1024, 64, 16)
        TOPK = NBLK // 4
        x_shape = x.shape
        xf = x.reshape(-1, IN_F)
        n = xf.shape[0]
        prob = jax.nn.softmax(xf @ router_w.T + router_b, axis=-1)
        _, idx = jax.lax.top_k(prob, TOPK)
        mask = jnp.zeros((n, NBLK), bool).at[jnp.arange(n)[:, None], idx].set(True)
        w1b = w1.reshape(NBLK, BLOCK, IN_F)
        b1b = b1.reshape(NBLK, BLOCK)
        h = jnp.einsum('nd,ibd->nib', xf, w1b) + b1b
        h = jnp.where(mask[:, :, None], h, jnp.zeros((), h.dtype))
        h = jax.nn.relu(h)
        w2b = w2.reshape(IN_F, NBLK, BLOCK)
        y = jnp.einsum('nib,dib->nd', jnp.where(mask[:, :, None], h, 0.0), w2b) + b2
        return y.reshape(x_shape)

    def _L1_xattn_ref(q, k, v, wq_w, wq_b, wk_w, wk_b, wv_w, wv_b, wo_w, wo_b):
        import jax, jax.numpy as jnp
        import numpy as np
        B, T, D, H = (2, 512, 256, 16)
        DH = D // H
        b, t, d = q.shape
        wq = (q @ wq_w.T + wq_b).reshape(b, t, H, DH)
        wk = (k @ wk_w.T + wk_b).reshape(b, t, H, DH)
        wv = (v @ wv_w.T + wv_b).reshape(b, t, H, DH)
        scores = jnp.einsum('bthd,bshd->bhts', wq, wk) / jnp.sqrt(jnp.float32(DH))
        probs = jax.nn.softmax(scores, axis=-1)
        attn = jnp.einsum('bhts,bshd->bthd', probs, wv)
        attn = attn.reshape(b, t, d)
        return attn @ wo_w.T + wo_b

    def _L1_ffn_ref(x, w1, b1, w2, b2):
        import jax, jax.numpy as jnp
        import numpy as np
        N_EMBD = 256
        N_STATE = 1024
        h = jax.nn.gelu(jnp.einsum('bse,eh->bsh', x, w1) + b1, approximate=False)
        return jnp.einsum('bsh,he->bse', h, w2) + b2
    x = x + _L0_xattn_ref(_layernorm(x, axis=-1), ctx_1024, ctx_1024, mask_1x1xSxS2_if1, L0_xattn_w_Q, L0_xattn_b_Q, L0_xattn_w_K, L0_xattn_b_K, L0_xattn_w_V, L0_xattn_b_V, L0_xattn_w_O, L0_xattn_b_O)
    x = x + _L0_ffn_ref(_layernorm(x, axis=-1), L0_ffn_router_w, L0_ffn_router_b, L0_ffn_w1, L0_ffn_b1, L0_ffn_w2, L0_ffn_b2)
    x = x + _L1_xattn_ref(_layernorm(x, axis=-1), ctx_1024, ctx_1024, L1_xattn_wq_w, L1_xattn_wq_b, L1_xattn_wk_w, L1_xattn_wk_b, L1_xattn_wv_w, L1_xattn_wv_b, L1_xattn_wo_w, L1_xattn_wo_b)
    x = x + _L1_ffn_ref(_layernorm(x, axis=-1), L1_ffn_w1, L1_ffn_b1, L1_ffn_w2, L1_ffn_b2)
    return x

_drawn_inputs = setup_inputs


def setup_inputs(seed=0):
    import zlib

    import numpy as np

    out = dict(_drawn_inputs(seed))
    spreads = {'L0_xattn_b_Q': (0.0, 0.415),
     'L0_xattn_b_K': (0.0, 0.8),
     'L0_xattn_b_V': (0.0, 0.1),
     'L0_xattn_b_O': (0.0, 0.1),
     'L1_xattn_wq_b': (0.0, 0.491),
     'L1_xattn_wk_b': (0.0, 0.8),
     'L1_xattn_wv_b': (0.0, 0.1),
     'L1_xattn_wo_b': (0.0, 0.1)}
    factors = {'L0_ffn_router_b': 2.95,
     'L0_ffn_b1': 8.0,
     'L0_ffn_b2': 4.353,
     'L1_ffn_b1': 6.869,
     'L1_ffn_b2': 4.7}
    for name, (base, spread) in spreads.items():
        noise = np.random.default_rng([zlib.crc32(name.encode()), seed]).standard_normal(out[name].shape)
        drawn = base * np.exp(spread * noise) if base else spread * noise
        out[name] = jnp.asarray(drawn.astype(out[name].dtype))
    for name, factor in factors.items():
        out[name] = (out[name] * factor).astype(out[name].dtype)
    return out
```

```python
from contextlib import ExitStack

import concourse.bass as bass
from concourse import mybir

P = 128
F32 = mybir.dt.float32
FR = mybir.dt.float32r
F16 = mybir.dt.float16
BF16 = mybir.dt.bfloat16
I32 = mybir.dt.int32
ALU = mybir.AluOpType
ACT = mybir.ActivationFunctionType
AX_X = mybir.AxisListType.X

H = 16
DH = 16
G = 4
EPS = 1e-5
MASK_BIG = float(2**19)
MAX_SCALE = 16.0
SCORE_ROWS = 112
MAX_ROW = SCORE_ROWS
MAX_SCALE_TWICE = 33632256.0
BLOCK_BIG = 1e30


def need(eng, sem, value, least):
    if least > 0:
        eng.wait_ge(sem, value)


def in_register(eng, value):
    return value if isinstance(value, int) else eng.to_reg(value)


def settle(eng, sem, value):
    eng.wait_ge(sem, value)


def stage_steps(n_steps, offsets):
    last = max(offsets) + n_steps
    ramp = max(offsets) + 2
    cuts = sorted({o + n_steps for o in offsets} | {last})
    ranges = [(t, t + 1) for t in range(ramp)]
    at = ramp
    for c in cuts:
        if c > at:
            ranges.append((at, c))
            at = c
    return ranges


def attention_phase(nc, layer, x_sb, ident_sb, stack, ins, scratch, scratch_w, B, S, D):
    NT = B * S // P
    TB = S // P
    KT = D // P
    VW = 2 * DH + 1
    OFF = dict(LN=0, PR=4, VP=6, SM=8, MR=9, PV=10, TL=11, OP=14)
    RANGES = stage_steps(NT, list(OFF.values()))

    def active(name, t0):
        return OFF[name] <= t0 < OFF[name] + NT

    with ExitStack() as ctx:
        ctx.enter_context(nc.cleanup_on_exit())

        def sb(name, shape, dt):
            return ctx.enter_context(nc.sbuf_tensor(f"L{layer}a_{name}", shape, dt))

        def sem(name):
            return nc.alloc_semaphore(name=f"L{layer}a_{name}")

        src = sb("src", [P, 2 * 2 * 2 * KT, S], FR)
        wqk = src[:, 0:4 * KT * P * 2 // S, :]
        wv = sb("wv", [P, 2, KT, D], FR)
        wo = sb("wo", [P, 2, KT, D], FR)
        wqk_now = sb("wqk_now", [P, 2 * KT, P], FR)
        vsrc = sb("vsrc", [P, 2 * KT, P], FR)
        osrc = sb("osrc", [P, D], F32)
        probs = sb("probs", [P, 2, TB, S], F32)
        plo = sb("plo", [P, 2, TB, S], F16)
        v16 = sb("v16", [P, 2 * TB * H, VW], F16)
        o_sb = sb("o_sb", [P, 2 * TB, D], F32)
        o_raw = sb("o_raw", [P, 2, TB, VW], F32)
        o_sum = sb("o_sum", [P, 2, TB, DH], F32)
        o_rec = sb("o_rec", [P, 2, TB], F32)
        oT = sb("oT", [P, 2, KT, P], FR)
        q32 = sb("q32", [P, S], F32)
        qhl = sb("qhl", [P, 2, S], F16)
        v32 = sb("v32", [P, D], F32)
        craw = sb("craw", [P, KT, P], F32)
        xn = sb("xn", [P, D], F32)
        stat = sb("stat", [P, 6], F32)
        mv = sb("mv", [P, 2], F32)
        rstd = sb("rstd", [P, 2], F32)
        half = sb("half", [P, 1], F32)
        maskT, keep = None, None
        if layer == 0:
            maskT = sb("maskT", [P, TB, S], BF16)
            keep = o_sb[:, :, :].bitcast(BF16).rearrange("p a d -> p (a d)").rearrange("p (a s) -> p a s", s=S)[:, 0:TB, :]
            mraw = plo[:, :, :, :].rearrange("p a b s -> p (a b s)").bitcast(I32).rearrange("p (a s) -> p a s", a=TB)
            kept = sb("kept", [P, 1], F32)
            kept_all = sb("kept_all", [1, 1], I32)
            onesb = sb("onesb", [P, P], BF16)
            onesf = sb("onesf", [P, P], F32)
        nmax = sb("nmax", [P, 2, G * TB], BF16)
        mrow = sb("mrow", [G * TB, P], F16)
        identb = sb("identb", [P, P], BF16)
        bqk = sb("bqk", [P, 4], F32)
        bv_b = sb("bv_b", [P, D], F32)
        bo_b = sb("bo_b", [P, D], F32)
        rowany = sb("rowany", [P, 2, S], BF16)

        ps_t = [ctx.enter_context(nc.psum_tensor(f"L{layer}a_ps_t{c}", [P, 2, S], F32)) for c in range(2)]
        ps_s = [ctx.enter_context(nc.psum_tensor(f"L{layer}a_ps_s{c}", [P, S], F32)) for c in range(2)]
        ps_o = ctx.enter_context(nc.psum_tensor(f"L{layer}a_ps_o", [P, 512], F32))
        ps_m = ctx.enter_context(nc.psum_tensor(f"L{layer}a_ps_m", [P, 512], F32))

        w_in = sem("w_in")
        w_st = sem("w_st")
        w_hi, w_lo = sem("w_hi"), sem("w_lo")
        x_in, c_in = sem("x_in"), sem("c_in")
        bn, mvd, var1, rsd, xnd = sem("bn"), sem("mvd"), sem("var1"), sem("rsd"), sem("xnd")
        xt, xhi, xlo = sem("xt"), sem("xhi"), sem("xlo")
        chi, clo = sem("chi"), sem("clo")
        xb = sem("xb")
        wnow, vnow, onow = sem("wnow"), sem("vnow"), sem("onow")
        prj, q32d, qhi, qlo = sem("prj"), sem("q32d"), sem("qhi"), sem("qlo")
        scr_w, stk = sem("scr_w"), sem("stk")
        vprj, v32d, vhi, vlo = sem("vprj"), sem("v32d"), sem("vhi"), sem("vlo")
        scq, smax = sem("scq"), sem("smax")
        mtr, mev, mdm = sem("mtr"), sem("mev"), sem("mdm")
        sck, pexp = sem("sck"), sem("pexp")
        plo_v, plo_g = sem("plo_v"), sem("plo_g")
        pv, oev, orc, oad, onm = sem("pv"), sem("oev"), sem("orc"), sem("oad"), sem("onm")
        otr, ohi, olo, oprj, xout = sem("otr"), sem("ohi"), sem("olo"), sem("oprj"), sem("xout")
        setup_g, setup_v, setup_w, setup_p = sem("setup_g"), sem("setup_v"), sem("setup_w"), sem("setup_p")
        N_LOADS = 11 if layer == 0 else 10
        G_SETUP = 9 if layer == 0 else 4
        V_SETUP = 10 if layer == 0 else 1

        wraw = probs[:, :, :, :].rearrange("p a b s -> p (a b s)")
        wraw_qk = wraw[:, 0:4 * KT * P].rearrange("p (m k c) -> p m k c", m=4, k=KT)
        wraw_v = wraw[:, 1024:1024 + KT * D].rearrange("p (k c) -> p k c", k=KT)
        wraw_o = wraw[:, 1536:1536 + KT * D].rearrange("p (k c) -> p k c", k=KT)
        wqk_v = wqk.rearrange("p a s -> p (a s)").rearrange("p (m h k c) -> p m h k c", m=4, h=2, k=KT)

        ctxT = ins["ctxT"].rearrange("(k p) t -> p k t", p=P)
        scr = scratch.rearrange("a h (j d) s -> (a h) d j s", d=DH)
        scr_out = scratch.rearrange("a h p s -> a p h s")

        USES = ["MR", "PR", "VP", "LN", "OT", "OP"]
        stage_of = dict(MR="MR", PR="PR", VP="VP", LN="LN", OT="OP", OP="OP")

        def uses(t0):
            return [u for u in USES if active(stage_of[u], t0)]

        read_out = dict(MR=mev, PR=q32d, VP=v32d, LN=xlo, OT=olo, OP=xout)

        def steps(eng, body):
            for t0, t1 in RANGES:
                if t1 - t0 == 1:
                    body(t0, t0)
                else:
                    with eng.Fori(t0, t1) as t:
                        body(t, t0)

        def parity(i):
            return (i // TB) % 2

        def batch_end(i):
            return TB * (i // TB) + TB

        def prior_batch(i):
            return TB * ((i - TB) // TB)

        block = ctx.enter_context(nc.Block())

        @block.sync
        def _(sp):
            if layer == 0:
                sp.dma_start(mraw, ins["maskT"].rearrange("(k p) q -> p k q", p=P)).then_inc(w_in, 16)
            for m in range(4):
                w = ins["wqT" if m % 2 == 0 else "wkT"].rearrange("(k p) c -> p k c", p=P)
                sp.dma_start(wraw_qk[:, m], w[:, :, (m // 2) * P:(m // 2 + 1) * P]).then_inc(w_in, 16)
            sp.dma_start(wraw_v, ins["wvT"].rearrange("(k p) c -> p k c", p=P)).then_inc(w_in, 16)
            sp.dma_start(wraw_o, ins["woT"].rearrange("(k p) c -> p k c", p=P)).then_inc(w_in, 16)
            sp.dma_start(bqk[:, 0:4:2], ins["bq"].rearrange("(m p) -> p m", p=P),
                         allow_slow_non_contiguous=True).then_inc(w_in, 16)
            sp.dma_start(bqk[:, 1:4:2], ins["bk"].rearrange("(m p) -> p m", p=P),
                         allow_slow_non_contiguous=True).then_inc(w_in, 16)
            sp.dma_start(bv_b[:, :], ins["bv"].partition_broadcast(P)).then_inc(w_in, 16)
            sp.dma_start(bo_b[:, :], ins["bo"].partition_broadcast(P)).then_inc(w_in, 16)

            sp.wait_ge(w_hi, 1)
            sp.wait_ge(w_lo, 1)
            sp.dma_start(scratch_w.rearrange("m p c -> p m c"), wqk_v.rearrange("p m h k c -> p m (h k c)").bitcast(F32)).then_inc(w_st, 16)
            sp.wait_ge(w_st, 16)

            def body(t, t0):
                i, j = t - OFF["PR"], t0 - OFF["PR"]
                if active("PR", t0):
                    before = in_register(sp, i)
                    settle(sp, w_st, 16)
                    need(sp, prj, before, j)
                    sp.dma_start(wqk_now[:, :, :].rearrange("p a c -> p (a c)").bitcast(F32),
                                 scratch_w[bass.ds(i % 4, 1)].rearrange("m p c -> (m p) c")).then_inc(wnow, 16)
                i, j = t - OFF["VP"], t0 - OFF["VP"]
                if active("VP", t0):
                    before, upto = in_register(sp, i), in_register(sp, i + 1)
                    settle(sp, w_st, 16)
                    need(sp, vprj, before, j)
                    sp.wait_ge(chi, upto)
                    sp.wait_ge(clo, upto)
                    sp.dma_start(vsrc[:, :, :].bitcast(F32), src[:, bass.ds(parity(i) * 8 + 4, 2 * KT), bass.ds((i % TB) * P, P)].bitcast(F32)).then_inc(vnow, 16)
                i, j = t - OFF["LN"], t0 - OFF["LN"]
                if active("LN", t0):
                    need(sp, clo, i, j)
                    if layer == 0:
                        need(sp, xnd, i, j)
                        sp.dma_start(x_sb[:, bass.ds(i, 1), :], ins["x"][:, bass.ds(i, 1), :]).then_inc(x_in, 16)
                    sp.dma_start(craw[:, :, :], ctxT[:, :, bass.ds(i * P, P)]).then_inc(c_in, 16)
                i, j = t - OFF["MR"], t0 - OFF["MR"]
                if active("MR", t0):
                    sp.wait_ge(mev, i + 1)
                    heads = parity(i) * 32 + ((i % 4) // 2) * 16 + (i % 2) * G
                    sp.dma_start(
                        stack[MAX_ROW:MAX_ROW + 1, bass.ds(heads, G), :].rearrange("o h (t q) -> o (h t) q", q=P),
                        mrow[:, :]).then_inc(mdm, 16)
                i, j = t - OFF["OP"], t0 - OFF["OP"]
                if active("OP", t0):
                    need(sp, otr, i, j)
                    sp.wait_ge(onm, G * batch_end(i))
                    sp.dma_start(osrc[:, :], o_sb[:, bass.ds(parity(i) * TB + i % TB, 1), :].rearrange("p a d -> p (a d)")).then_inc(onow, 16)
                i, j = t - OFF["PR"], t0 - OFF["PR"]
                if active("PR", t0):
                    stacked, upto = in_register(sp, 48 * i), in_register(sp, i + 1)
                    settle(sp, w_st, 16)
                    need(sp, stk, stacked, 48 * j)
                    sp.wait_ge(qhi, upto)
                    sp.wait_ge(qlo, upto)
                    sp.dma_start(scr_out[bass.ds(i % 2, 1)].rearrange("a p h s -> (a p) h s"), qhl[:, :, :]).then_inc(scr_w, 16)
                    scored = in_register(sp, 8 * (4 * ((i - 8) // 4) + 2 * ((i % 4) // 2) + 2))
                    written = in_register(sp, 16 * (i + 1))
                    settle(sp, w_st, 16)
                    need(sp, sck, scored, 8 * (4 * ((j - 8) // 4) + 2 * ((j % 4) // 2) + 2))
                    sp.wait_ge(scr_w, written)
                    dst = bass.ds((i % 8) * 8, 8)
                    is_k = i % 2
                    for r, half_no in enumerate([0, is_k, 1 - is_k]):
                        sp.dma_start(stack[r * DH:(r + 1) * DH, dst, :],
                                     scr[bass.ds(2 * (i % 2) + half_no, 1)].rearrange("a d j s -> (a d) j s")).then_inc(stk, 16)

            steps(sp, body)
            sp.wait_ge(scr_w, 16 * NT)
            sp.wait_ge(stk, 48 * NT)

        @block.tensor
        def _(pe):
            def split3(out, lhs, rhs, n):
                pairs = [(a, b, k) for a, b in ((0, 0), (0, 1), (1, 0)) for k in range(n)]
                for m, (a, b, k) in enumerate(pairs):
                    last = pe.matmul(out, lhs(a, k), rhs(b, k), start=(m == 0), stop=(m == len(pairs) - 1))
                return last

            def build(masked):
                def one_score(out, rows, a, b, at, mask_parts):
                    last = pe.matmul(out, stack[0:rows, bass.ds(a, 1), at * P:(at + 1) * P].rearrange("p a s -> p (a s)"),
                                     stack[0:rows, bass.ds(b, 1), :].rearrange("p a s -> p (a s)"),
                                     start=True, stop=not masked)
                    if masked:
                        for m, (o, lhs, rhs) in enumerate(mask_parts):
                            last = pe.matmul(o, lhs, rhs, start=False, stop=(m == len(mask_parts) - 1))
                    return last

                def q_head(i, hh):
                    return parity(i) * 32 + ((i % 4) // 2) * 16 + (i % 2) * G + hh

                def scores_q(t, t0, hh, tiles):
                    i, j = t - OFF["SM"], t0 - OFF["SM"]
                    if not active("SM", t0):
                        return
                    if hh == 0 and tiles[0] == 0:
                        pe.wait_ge(stk, 48 * batch_end(i))
                    for qt in tiles:
                        n, n0 = 16 * i + 4 * hh + qt, 16 * j + 4 * hh + qt
                        need(pe, smax, n - 1, n0 - 1)
                        out = ps_s[qt % 2]
                        parts = [(out[:, kt * P:(kt + 1) * P], maskT[:, kt, qt * P:(qt + 1) * P], identb[:, :])
                                 for kt in range(TB)] if masked else []
                        one_score(out[:, :], SCORE_ROWS, q_head(i, hh), q_head(i, hh) + 8, qt, parts).then_inc(scq, 1)

                def scores_k(t, t0, hh, c):
                    i, j = t - OFF["PV"], t0 - OFF["PV"]
                    if not active("PV", t0):
                        return
                    if hh == 0 and c == 0:
                        pe.wait_ge(mdm, 16 * (i + 1))
                    m, m0 = G * i + hh, G * j + hh
                    need(pe, pexp, 2 * m + c - 1, 2 * m0 + c - 1)
                    for kk in range(2):
                        kt = 2 * c + kk
                        parts = [(ps_t[c][:, kk, :], identb[:, :], maskT[:, kt, :])] if masked else []
                        last = one_score(ps_t[c][:, kk, :], MAX_ROW + 1, q_head(i, hh) + 8, q_head(i, hh), kt, parts)
                    last.then_inc(sck, 1)

                def times_v(i, j, hh):
                    m, m0 = G * i + hh, G * j + hh
                    pe.wait_ge(plo_v, m + 1)
                    pe.wait_ge(plo_g, m + 1)
                    need(pe, oev, m, m0)
                    if hh == 0:
                        pe.wait_ge(vhi, batch_end(i))
                        pe.wait_ge(vlo, batch_end(i))
                    hi = probs[:, hh % 2, :, :].bitcast(BF16)
                    for qt in range(TB):
                        for kt in range(TB):
                            for part in range(2):
                                if part == 0:
                                    lhs = hi[:, kt, 2 * qt * P + 1:2 * (qt + 1) * P:2]
                                else:
                                    lhs = plo[:, hh % 2, kt, qt * P:(qt + 1) * P]
                                v_at = parity(i) * TB * H + kt * H + (i % 4) * G + hh
                                last = pe.matmul(ps_o[:, qt * VW:(qt + 1) * VW], lhs,
                                                 v16[:, bass.ds(v_at, 1), :].rearrange("p a w -> p (a w)"),
                                                 start=(kt == 0 and part == 0), stop=(kt == TB - 1 and part == 1))
                    last.then_inc(pv, 1)

                def shared(name, t, t0):
                    at = uses(t0).index(name)
                    if at > 0:
                        before = uses(t0)[at - 1]
                        pe.wait_ge(read_out[before], t - OFF[stage_of[before]] + 1)
                        return
                    at_range = [r[0] for r in RANGES].index(t0)
                    if at_range > 0:
                        before = uses(RANGES[at_range - 1][0])[-1]
                        pe.wait_ge(read_out[before], t0 - OFF[stage_of[before]])
                    before = uses(t0)[-1]
                    if t is not t0 and t0 >= OFF[stage_of[before]]:
                        pe.wait_ge(read_out[before], t - OFF[stage_of[before]])

                def max_rows(t, t0):
                    if active("MR", t0):
                        i = t - OFF["MR"]
                        pe.wait_ge(smax, 16 * (i + 1))
                        shared("MR", t, t0)
                        pe.matmul(ps_m[0:G * TB, 0:P], nmax[:, bass.ds(i % 2, 1), :].rearrange("p a c -> p (a c)"),
                                  identb[:, :], start=True, stop=True).then_inc(mtr, 1)

                def project(t, t0):
                    if active("PR", t0):
                        i = t - OFF["PR"]
                        for s in (xhi, xlo, chi, clo):
                            pe.wait_ge(s, batch_end(i))
                        pe.wait_ge(wnow, 16 * (i + 1))
                        shared("PR", t, t0)
                        base = parity(i) * 8 + (i % 2) * 4
                        split3(ps_m[:, :], lambda a, k: wqk_now[:, a * KT + k, :],
                               lambda b, k: src[:, bass.ds(base + b * KT + k, 1), :].rearrange("p a s -> p (a s)"), KT).then_inc(prj, 1)

                def project_v(t, t0):
                    if active("VP", t0):
                        i = t - OFF["VP"]
                        pe.wait_ge(vnow, 16 * (i + 1))
                        shared("VP", t, t0)
                        split3(ps_m[:, 0:D], lambda a, k: vsrc[:, a * KT + k, :], lambda b, k: wv[:, b, k, :], KT).then_inc(vprj, 1)

                def turn_x(t, t0):
                    if active("LN", t0):
                        i = t - OFF["LN"]
                        pe.wait_ge(xnd, i + 1)
                        shared("LN", t, t0)
                        for k in range(KT):
                            last = pe.transpose(ps_m[:, k * P:(k + 1) * P], xn[:, k * P:(k + 1) * P], ident_sb[:, :])
                        last.then_inc(xt, 1)

                def turn_o(t, t0):
                    if active("OP", t0):
                        i = t - OFF["OP"]
                        pe.wait_ge(onow, 16 * (i + 1))
                        shared("OT", t, t0)
                        for k in range(KT):
                            last = pe.transpose(ps_m[:, k * P:(k + 1) * P], osrc[:, k * P:(k + 1) * P], ident_sb[:, :])
                        last.then_inc(otr, 1)

                def project_o(t, t0):
                    if active("OP", t0):
                        i = t - OFF["OP"]
                        pe.wait_ge(ohi, i + 1)
                        pe.wait_ge(olo, i + 1)
                        shared("OP", t, t0)
                        split3(ps_m[:, 0:D], lambda a, k: oT[:, a, k, :], lambda b, k: wo[:, b, k, :], KT).then_inc(oprj, 1)

                def body(t, t0):
                    for hh in range(G):
                        scores_k(t, t0, hh, 0)
                        scores_q(t, t0, hh, (0, 1))
                        if hh == 1:
                            project(t, t0)
                        if hh == 2:
                            project_v(t, t0)
                        if hh == 3:
                            turn_o(t, t0)
                        scores_k(t, t0, hh, 1)
                        scores_q(t, t0, hh, (2, 3))
                        if hh == 0:
                            if active("TL", t0):
                                times_v(t - OFF["TL"], t0 - OFF["TL"], G - 1)
                            max_rows(t, t0)
                        elif active("PV", t0):
                            times_v(t - OFF["PV"], t0 - OFF["PV"], hh - 1)
                        if hh == 2:
                            turn_x(t, t0)
                        if hh == 3:
                            project_o(t, t0)

                return body

            if layer == 0:
                pe.wait_ge(setup_v, 1)
                pe.wait_ge(setup_g, 5)
                for kt in range(TB):
                    last = pe.matmul(ps_m[:, :], onesb[:, :], keep[:, kt, :], start=(kt == 0), stop=(kt == TB - 1))
                last.then_inc(setup_p, 1)
                pe.wait_ge(setup_v, 2)
                pe.matmul(ps_o[:, 0:1], onesf[:, :], kept[:, :], start=True, stop=True).then_inc(setup_p, 1)
                pe.wait_ge(setup_v, V_SETUP)
                kept_count = pe.value_load(kept_all[0:1, 0:1], min_val=0, max_val=S * S)
                with pe.If(kept_count < S * S):
                    steps(pe, build(True))
                with pe.Else():
                    steps(pe, build(False))
            else:
                pe.wait_ge(setup_g, G_SETUP)
                pe.wait_ge(setup_v, V_SETUP)
                steps(pe, build(False))

        @block.scalar
        def _(act):
            act.wait_ge(w_in, N_LOADS * 16)
            act.copy(wqk_v[:, :, 0], wraw_qk).then_inc(w_hi, 1)
            act.copy(wv[:, 0], wraw_v).then_inc(w_hi, 1)
            act.copy(wo[:, 0], wraw_o).then_inc(w_hi, 1)
            act.wait_ge(w_lo, 3)
            act.wait_ge(w_st, 16)

            def exponentials(t, t0, hh, c):
                i, j = t - OFF["PV"], t0 - OFF["PV"]
                if active("PV", t0):
                    m, m0 = G * i + hh, G * j + hh
                    act.wait_ge(sck, 2 * m + c + 1)
                    need(act, pv, m - 1, m0 - 1)
                    act.activation(probs[:, hh % 2, 2 * c:2 * c + 2, :], ps_t[c][:, :, :], ACT.Exp,
                                   scale=1.0 / DH**0.5).then_inc(pexp, 1)

            def take_o(i, j, hh):
                m, m0 = G * i + hh, G * j + hh
                act.wait_ge(pv, m + 1)
                need(act, onm, m - 1, m0 - 1)
                act.copy(o_raw[:, hh % 2, :, :], ps_o[:, 0:TB * VW].rearrange("p (a w) -> p a w", a=TB)).then_inc(oev, 1)

            def body(t, t0):
                for hh in range(G):
                    exponentials(t, t0, hh, 0)
                    if hh == 2 and active("PR", t0):
                        i, j = t - OFF["PR"], t0 - OFF["PR"]
                        act.wait_ge(q32d, i + 1)
                        need(act, scr_w, 16 * i, 16 * j)
                        act.copy(qhl[:, 0, :], q32[:, :]).then_inc(qhi, 1)
                    if hh == 3 and active("LN", t0):
                        i, j = t - OFF["LN"], t0 - OFF["LN"]
                        act.wait_ge(xt, i + 1)
                        need(act, prj, prior_batch(i), prior_batch(j))
                        act.copy(src[:, bass.ds(parity(i) * 8, KT), bass.ds((i % TB) * P, P)],
                                 ps_m[:, 0:D].rearrange("p (k c) -> p k c", k=KT)).then_inc(xhi, 1)
                    exponentials(t, t0, hh, 1)
                    if hh == 0:
                        if active("TL", t0):
                            take_o(t - OFF["TL"], t0 - OFF["TL"], G - 1)
                        if active("MR", t0):
                            i, j = t - OFF["MR"], t0 - OFF["MR"]
                            act.wait_ge(mtr, i  + 1)
                            need(act, mdm, 16 * i, 16 * j)
                            act.activation(mrow[:, :], ps_m[0:G * TB, 0:P], ACT.Copy, scale=-1.0 / MAX_SCALE).then_inc(mev, 1)
                    elif active("PV", t0):
                        take_o(t - OFF["PV"], t0 - OFF["PV"], hh - 1)
                    if hh == 0 and active("LN", t0):
                        i, j = t - OFF["LN"], t0 - OFF["LN"]
                        act.wait_ge(c_in, 16 * (i + 1))
                        need(act, prj, prior_batch(i), prior_batch(j))
                        need(act, vnow, 16 * (i - 7), 16 * (j - 7))
                        at = parity(i) * 8 + 4
                        act.copy(src[:, bass.ds(at, KT), bass.ds((i % TB) * P, P)], craw[:, :, :]).then_inc(chi, 1)
                    if hh == 2 and active("VP", t0):
                        i, j = t - OFF["VP"], t0 - OFF["VP"]
                        act.wait_ge(v32d, i + 1)
                        need(act, pv, 4 * G * ((i - TB) // TB), 4 * G * ((j - TB) // TB))
                        act.copy(v16[:, bass.ds(parity(i) * TB * H + (i % TB) * H, H), 0:DH],
                                 v32[:, :].rearrange("p (h d) -> p h d", d=DH)).then_inc(vhi, 1)
                    if hh == 3 and active("OP", t0):
                        i, j = t - OFF["OP"], t0 - OFF["OP"]
                        act.wait_ge(otr, i + 1)
                        need(act, oprj, i, j)
                        act.copy(oT[:, 0], ps_m[:, 0:D].rearrange("p (k c) -> p k c", k=KT)).then_inc(ohi, 1)

            steps(act, body)

        @block.vector
        def _(dve):
            if layer == 0:
                dve.memset(rowany[:, 1, :], 1.0).then_inc(setup_w, 1)
                dve.wait_ge(w_in, N_LOADS * 16)
                dve.tensor_scalar(keep, mraw, 0.0, None, ALU.not_equal).then_inc(setup_v, 1)
                dve.wait_ge(setup_v, 1)
                dve.tensor_reduce(kept[:, :], keep.rearrange("p a s -> p (a s)"), AX_X, ALU.add).then_inc(setup_v, 1)
                dve.wait_ge(setup_p, 1)
                dve.tensor_scalar(rowany[:, 0, :], ps_m[:, :], 1.0, None, ALU.min).then_inc(setup_v, 1)
                dve.tensor_scalar(maskT[:, :, :], keep, 1.0, MASK_BIG, ALU.subtract, ALU.mult).then_inc(setup_v, 1)
                dve.wait_ge(setup_v, 4)
                for kt in range(TB):
                    dve.tensor_tensor(maskT[:, kt, :], maskT[:, kt, :], rowany[:, 0, :], ALU.mult).then_inc(setup_v, 1)
                dve.wait_ge(setup_p, 2)
                dve.tensor_copy(kept_all[:, :], ps_o[0:1, 0:1]).then_inc(setup_v, 1)
                q_rows = stack[:, :, :].bitcast(F32).rearrange("p (a k h) s -> p a k (h s)", k=2, h=8)[:, :, 0, :]
                dve.memset(q_rows, 0.0).then_inc(setup_v, 1)
            else:
                dve.memset(rowany[:, :, :].rearrange("p a s -> p (a s)"), 1.0).then_inc(setup_v, 1)
                dve.wait_ge(w_in, N_LOADS * 16)
            dve.wait_ge(setup_v, V_SETUP)
            dve.wait_ge(w_hi, 1)
            dve.tensor_tensor(wqk_v[:, :, 1], wraw_qk, wqk_v[:, :, 0].bitcast(F32), ALU.subtract).then_inc(w_lo, 1)
            dve.wait_ge(w_hi, 2)
            dve.tensor_tensor(wv[:, 1], wraw_v, wv[:, 0].bitcast(F32), ALU.subtract).then_inc(w_lo, 1)
            dve.wait_ge(w_hi, 3)
            dve.tensor_tensor(wo[:, 1], wraw_o, wo[:, 0].bitcast(F32), ALU.subtract).then_inc(w_lo, 1)
            if layer == 0:
                dve.wait_ge(setup_w, 1)

            def maxima(t, t0, hh, tiles):
                i, j = t - OFF["SM"], t0 - OFF["SM"]
                if active("SM", t0):
                    for qt in tiles:
                        dve.wait_ge(scq, 16 * i + 4 * hh + qt + 1)
                        need(dve, mtr, i - 1 , j - 1)
                        col = hh * TB + qt
                        dve.tensor_reduce(nmax[:, bass.ds(i % 2, 1), col:col + 1].rearrange("p a c -> p (a c)"),
                                          ps_s[qt % 2][:, :], AX_X, ALU.max).then_inc(smax, 1)

            def remainder(t, t0, hh):
                i, j = t - OFF["PV"], t0 - OFF["PV"]
                if active("PV", t0):
                    m, m0 = G * i + hh, G * j + hh
                    dve.wait_ge(pexp, 2 * m + 1)
                    p = probs[:, hh % 2, 0:2, :].rearrange("p a s -> p (a s)")
                    dve.tensor_tensor(plo[:, hh % 2, 0:2, :].rearrange("p a s -> p (a s)"), p,
                                      p.bitcast(BF16)[:, 1::2], ALU.subtract).then_inc(plo_v, 1)

            def reciprocal(i, j, hh):
                m, m0 = G * i + hh, G * j + hh
                dve.wait_ge(oev, m + 1)
                need(dve, onm, m - 1, m0 - 1)
                dve.reciprocal(o_rec[:, hh % 2, :], o_raw[:, hh % 2, :, 2 * DH]).then_inc(orc, 1)

            def body(t, t0):
                for hh in range(G):
                    maxima(t, t0, hh, (0, 1))
                    remainder(t, t0, hh)
                    if hh == 1 and active("PR", t0):
                        i, j = t - OFF["PR"], t0 - OFF["PR"]
                        dve.wait_ge(prj, i + 1)
                        need(dve, qhi, i, j)
                        need(dve, qlo, i, j)
                        dve.scalar_tensor_tensor(out=q32[:, :], in0=ps_m[:, :], scalar=bqk[:, bass.ds(i % 4, 1)],
                                                 in1=rowany[:, bass.ds(i % 2, 1), :].rearrange("p a s -> p (a s)"),
                                                 op0=ALU.add, op1=ALU.mult).then_inc(q32d, 1)
                    if hh == 2 and active("VP", t0):
                        i, j = t - OFF["VP"], t0 - OFF["VP"]
                        dve.wait_ge(vprj, i + 1)
                        need(dve, vlo, i, j)
                        need(dve, vhi, i, j)
                        dve.tensor_tensor(v32[:, :], ps_m[:, 0:D], bv_b[:, :], ALU.add).then_inc(v32d, 1)
                    if hh == 3 and active("LN", t0):
                        i, j = t - OFF["LN"], t0 - OFF["LN"]
                        dve.wait_ge(xhi, i + 1)
                        at = bass.ds(parity(i) * 8, KT)
                        to = bass.ds(parity(i) * 8 + KT, KT)
                        cols = bass.ds((i % TB) * P, P)
                        dve.tensor_tensor(src[:, to, cols], ps_m[:, 0:D].rearrange("p (k c) -> p k c", k=KT),
                                          src[:, at, cols].bitcast(F32), ALU.subtract).then_inc(xlo, 1)
                    maxima(t, t0, hh, (2, 3))
                    if hh == 0:
                        if active("TL", t0):
                            reciprocal(t - OFF["TL"], t0 - OFF["TL"], G - 1)
                    elif active("PV", t0):
                        reciprocal(t - OFF["PV"], t0 - OFF["PV"], hh - 1)
                    i, j = t - OFF["LN"], t0 - OFF["LN"]
                    if hh == 0 and active("LN", t0):
                        if layer == 0:
                            dve.wait_ge(x_in, 16 * (i + 1))
                        need(dve, mvd, i, j)
                        dve.bn_stats(stat[:, :], x_sb[:, bass.ds(i, 1), :].rearrange("p a d -> p (a d)")).then_inc(bn, 1)
                        upto = in_register(dve, i + 1)
                        settle(dve, w_in, N_LOADS * 16)
                        dve.wait_ge(bn, upto)
                        need(dve, xnd, i, j)
                        need(dve, var1, i, j)
                        dve.bn_aggr(mv[:, :], stat[:, :]).then_inc(mvd, 1)
                    if hh == 1 and active("LN", t0):
                        dve.wait_ge(rsd, i + 1)
                        need(dve, xt, i, j)
                        dve.tensor_scalar(xn[:, :], x_sb[:, bass.ds(i, 1), :].rearrange("p a d -> p (a d)"),
                                          mv[:, 0:1], rstd[:, 1:2], ALU.subtract, ALU.mult).then_inc(xnd, 1)
                    i, j = t - OFF["OP"], t0 - OFF["OP"]
                    if hh == 3 and active("OP", t0):
                        dve.wait_ge(ohi, i + 1)
                        dve.tensor_tensor(oT[:, 1], ps_m[:, 0:D].rearrange("p (k c) -> p k c", k=KT),
                                          oT[:, 0].bitcast(F32), ALU.subtract).then_inc(olo, 1)
                        dve.wait_ge(oprj, i + 1)
                        dve.wait_ge(xb, i + 1)
                        xi = x_sb[:, bass.ds(i, 1), :].rearrange("p a d -> p (a d)")
                        dve.tensor_tensor(xi, ps_m[:, 0:D], xi, ALU.add).then_inc(xout, 1)

            steps(dve, body)

        @block.gpsimd
        def _(pool):
            pool.memset(half[:, :], -0.5).then_inc(setup_g, 1)
            pool.memset(v16[:, :, :].rearrange("p a w -> p (a w)"), 1.0).then_inc(setup_g, 1)
            pool.memset(identb[:, :], 0.0).then_inc(setup_g, 1)
            if layer == 0:
                pool.memset(onesb[:, :], 1.0).then_inc(setup_g, 1)
                pool.memset(onesf[:, :], 1.0).then_inc(setup_g, 1)
                pool.memset(ident_sb[:, :], 0.0).then_inc(setup_g, 1)
                k_rows = stack[:, :, :].bitcast(F32).rearrange("p (a k h) s -> p a k (h s)", k=2, h=8)[:, :, 1, :]
                pool.memset(k_rows, MAX_SCALE_TWICE).then_inc(setup_g, 1)
                pool.wait_ge(setup_g, 6)
                pool.affine_select(out=ident_sb[:, :], in_=ident_sb[:, :], compare_op=ALU.not_equal, fill=1.0,
                                   base=0, pattern=[[-1, P]], channel_multiplier=1).then_inc(setup_g, 1)
            pool.wait_ge(setup_g, 3)
            pool.affine_select(out=identb[:, :], in_=identb[:, :], compare_op=ALU.not_equal, fill=1.0,
                               base=0, pattern=[[-1, P]], channel_multiplier=1).then_inc(setup_g, 1)
            pool.wait_ge(setup_g, G_SETUP)
            pool.wait_ge(w_in, N_LOADS * 16)

            def remainder(t, t0, hh):
                i, j = t - OFF["PV"], t0 - OFF["PV"]
                if active("PV", t0):
                    m = G * i + hh
                    pool.wait_ge(pexp, 2 * m + 2)
                    p = probs[:, hh % 2, 2:4, :].rearrange("p a s -> p (a s)")
                    pool.tensor_tensor(plo[:, hh % 2, 2:4, :].rearrange("p a s -> p (a s)"), p,
                                       p.bitcast(BF16)[:, 1::2], ALU.subtract).then_inc(plo_g, 1)

            def normalise(i, j, hh):
                m, m0 = G * i + hh, G * j + hh
                pool.wait_ge(oev, m + 1)
                need(pool, onm, m - 1, m0 - 1)
                pool.tensor_tensor(o_sum[:, hh % 2], o_raw[:, hh % 2, :, 0:DH], o_raw[:, hh % 2, :, DH:2 * DH],
                                   ALU.add).then_inc(oad, 1)
                pool.wait_ge(oad, m + 1)
                pool.wait_ge(orc, m + 1)
                need(pool, onow, 16 * prior_batch(i), 16 * prior_batch(j))
                head = (i % 4) * G + hh
                pool.tensor_tensor(o_sb[:, bass.ds(parity(i) * TB, TB), bass.ds(head * DH, DH)], o_sum[:, hh % 2],
                                   o_rec[:, hh % 2, :].unsqueeze(2).to_broadcast([P, TB, DH]), ALU.mult).then_inc(onm, 1)

            def body(t, t0):
                for hh in range(G):
                    if hh == 0:
                        i, j = t - OFF["LN"], t0 - OFF["LN"]
                        if active("LN", t0):
                            upto = in_register(pool, i + 1)
                            settle(pool, w_in, N_LOADS * 16)
                            pool.wait_ge(mvd, upto)
                            need(pool, xnd, i, j)
                            pool.tensor_scalar(rstd[:, 0:1], mv[:, 1:2], EPS, None, ALU.add).then_inc(var1, 1)
                            pool.wait_ge(var1, i + 1)
                            pool.tensor_tensor(rstd[:, 1:2], rstd[:, 0:1], half[:, :], ALU.pow).then_inc(rsd, 1)
                    remainder(t, t0, hh)
                    if hh == 0:
                        if active("TL", t0):
                            normalise(t - OFF["TL"], t0 - OFF["TL"], G - 1)
                        i, j = t - OFF["LN"], t0 - OFF["LN"]
                        if active("LN", t0):
                            pool.wait_ge(chi, i + 1)
                            at = bass.ds(parity(i) * 8 + 4, KT)
                            to = bass.ds(parity(i) * 8 + 4 + KT, KT)
                            cols = bass.ds((i % TB) * P, P)
                            pool.tensor_tensor(src[:, to, cols], craw[:, :, :], src[:, at, cols].bitcast(F32),
                                               ALU.subtract).then_inc(clo, 1)
                    elif active("PV", t0):
                        normalise(t - OFF["PV"], t0 - OFF["PV"], hh - 1)
                    i, j = t - OFF["LN"], t0 - OFF["LN"]
                    if hh == 1 and active("LN", t0):
                        pool.wait_ge(xnd, i + 1)
                        xi = x_sb[:, bass.ds(i, 1), :].rearrange("p a d -> p (a d)")
                        pool.tensor_tensor(xi, xi, bo_b[:, :], ALU.add).then_inc(xb, 1)
                    i, j = t - OFF["PR"], t0 - OFF["PR"]
                    if hh == 2 and active("PR", t0):
                        pool.wait_ge(qhi, i + 1)
                        pool.tensor_tensor(qhl[:, 1, :], q32[:, :], qhl[:, 0, :], ALU.subtract).then_inc(qlo, 1)
                    i, j = t - OFF["VP"], t0 - OFF["VP"]
                    if hh == 3 and active("VP", t0):
                        pool.wait_ge(vhi, i + 1)
                        heads = bass.ds(parity(i) * TB * H + (i % TB) * H, H)
                        pool.tensor_tensor(v16[:, heads, DH:2 * DH], v32[:, :].rearrange("p (h d) -> p h d", d=DH),
                                           v16[:, heads, 0:DH], ALU.subtract).then_inc(vlo, 1)

            steps(pool, body)


def ffn_phase(nc, layer, x_sb, ident_sb, ins, out, B, S, D, FF):
    TB = S // P
    KT = D // P
    NC = FF // P
    NB = 16
    TOPK = NB // 4
    ROUNDS = TB // 2
    OFF = dict(LN=0, MM=1, YT=2)
    RANGES = [(t, t + 1) for t in range(3)] + ([(3, B)] if B > 3 else [])
    RANGES += [(t, t + 1) for t in range(max(B, 3), B + 2)]

    def active(name, t0):
        return OFF[name] <= t0 < OFF[name] + B

    with ExitStack() as ctx:
        ctx.enter_context(nc.cleanup_on_exit())

        def sb(name, shape, dt):
            return ctx.enter_context(nc.sbuf_tensor(f"L{layer}f_{name}", shape, dt))

        def pb(name, shape, dt):
            return ctx.enter_context(nc.psum_tensor(f"L{layer}f_{name}", shape, dt))

        def sem(name):
            return nc.alloc_semaphore(name=f"L{layer}f_{name}")

        w1 = sb("w1", [P, 2, KT, FF], FR)
        w2 = sb("w2", [P, 2, NC, D], FR)
        w1raw = sb("w1raw", [P, KT, FF], F32)
        w2raw = sb("w2raw", [P, NC, D], F32)
        b1 = sb("b1", [P, NC], F32)
        b2_b = sb("b2_b", [P, 1, D], F32)
        stat = sb("stat", [P, TB, 6], F32)
        mv = sb("mv", [P, TB, 2], F32)
        rstd = sb("rstd", [P, 2, TB], F32)
        half = sb("half", [P, TB], F32)
        xn = sb("xn", [P, TB, D], F32)
        xnT = sb("xnT", [P, 2 * 2 * KT, S], FR)
        h32 = sb("h32", [P, 2, S], F32)
        hT = sb("hT", [P, 2, 2, S], FR)
        if layer == 0:
            rwraw = sb("rwraw", [P, KT, NB], F32)
            rw = sb("rw", [P, 2, KT, NB], FR)
            rb = sb("rb", [NB, 1], F32)
            lgT = sb("lgT", [NB, S], F32)
            lg = sb("lg", [P, TB, NB], F32)
            top8 = sb("top8", [P, TB, 8], F32)
            marked = sb("marked", [P, TB, NB], F32)
            pen = sb("pen", [P, TB, NB], BF16)
            penT = sb("penT", [P, 2, S], BF16)
            spread = sb("spread", [P, FF], BF16)
            identb = sb("identb", [P, P], BF16)

        ps_h = [pb(f"ps_h{c}", [P, S], F32) for c in range(2)]
        ps_y = [pb(f"ps_y{c}", [P, 2, D], F32) for c in range(ROUNDS)]
        ps_x = [pb(f"ps_x{c}", [P, 2, KT, P], F32) for c in range(ROUNDS)]
        if layer == 0:
            ps_r = pb("ps_r", [P, S], F32)
            ps_q = pb("ps_q", [P, 512], F32)
            ps_pen = ps_r[:, :].bitcast(BF16)

        w_in, w_hi, w_lo, const = sem("w_in"), sem("w_hi"), sem("w_lo"), sem("const")
        bn, mvd, var1, rsd, xnd = sem("bn"), sem("mvd"), sem("var1"), sem("rsd"), sem("xnd")
        xt, xhi, xlo, xb = sem("xt"), sem("xhi"), sem("xlo"), sem("xb")
        lgp, lge, lgt, lgc = sem("lgp"), sem("lge"), sem("lgt"), sem("lgc")
        top, abs8, mrk, pnd, pnt, pne = sem("top"), sem("abs8"), sem("mrk"), sem("pnd"), sem("pnt"), sem("pne")
        hp, h32d, hhi, hlo = sem("hp"), sem("h32d"), sem("hhi"), sem("hlo")
        yp, yout = sem("yp"), sem("yout")
        stored = sem("stored")
        N_LOADS = 6 if layer == 0 else 4
        N_SPLITS = 3 if layer == 0 else 2
        N_CONST = 7 if layer == 0 else 1

        def steps(eng, body):
            for t0, t1 in RANGES:
                if t1 - t0 == 1:
                    body(t0, t0)
                else:
                    with eng.Fori(t0, t1) as t:
                        body(t, t0)

        def parity(i):
            return i % 2

        block = ctx.enter_context(nc.Block())

        @block.sync
        def _(sp):
            sp.dma_start(w1raw[:, :, :], ins["w1"].rearrange("(k p) c -> p k c", p=P)).then_inc(w_in, 16)
            sp.dma_start(w2raw[:, :, :], ins["w2"].rearrange("(k p) c -> p k c", p=P)).then_inc(w_in, 16)
            sp.dma_start(b1[:, :], ins["b1"].rearrange("(m p) -> p m", p=P),
                         allow_slow_non_contiguous=True).then_inc(w_in, 16)
            sp.dma_start(b2_b[:, 0, :], ins["b2"].partition_broadcast(P)).then_inc(w_in, 16)
            if layer == 0:
                sp.dma_start(rwraw[:, :, :], ins["rw"].rearrange("(k p) c -> p k c", p=P)).then_inc(w_in, 16)
                sp.dma_start(rb[:, :], ins["rb"].rearrange("(p o) -> p o", o=1)).then_inc(w_in, 16)

            def body(t, t0):
                if out is not None and active("YT", t0):
                    i = t - OFF["YT"]
                    sp.wait_ge(yout, ROUNDS * (i + 1))
                    sp.dma_start(out[:, bass.ds(i * TB, TB), :], x_sb[:, bass.ds(i * TB, TB), :]).then_inc(stored, 16)

            if out is not None:
                steps(sp, body)
                sp.wait_ge(stored, 16 * B)

        @block.tensor
        def _(pe):
            def split3(out_ap, lhs, rhs, n, more=False, **flags):
                pairs = [(a, b, k) for a, b in ((0, 0), (0, 1), (1, 0)) for k in range(n)]
                for m, (a, b, k) in enumerate(pairs):
                    last = pe.matmul(out_ap, lhs(a, k), rhs(b, k), start=(m == 0), stop=(m == len(pairs) - 1 and not more))
                return last

            def turned(i, b, k):
                return xnT[:, bass.ds(parity(i) * 2 * KT + b * KT + k, 1), :].rearrange("p a s -> p (a s)")

            def first_product(i, j, c):
                n, n0 = NC * i + c, NC * j + c
                if c == 0:
                    pe.wait_ge(xhi, ROUNDS * (i + 1))
                    pe.wait_ge(xlo, ROUNDS * (i + 1))
                    if layer == 0:
                        pe.wait_ge(pne, i + 1)
                need(pe, h32d, n - 1, n0 - 1)
                last = split3(ps_h[c % 2][:, :], lambda a, k: w1[:, a, k, c * P:(c + 1) * P],
                              lambda b, k: turned(i, b, k), KT, more=(layer == 0))
                if layer == 0:
                    last = pe.matmul(ps_h[c % 2][:, :], spread[:, c * P:(c + 1) * P],
                                     penT[:, bass.ds(parity(i), 1), :].rearrange("p a s -> p (a s)"), start=False, stop=True)
                last.then_inc(hp, 1)

            def second_product(i, j, c):
                n = NC * i + c
                pe.wait_ge(hhi, n + 1)
                pe.wait_ge(hlo, n + 1)
                if c == 0:
                    need(pe, yout, ROUNDS * i, ROUNDS * j)
                for tt in range(TB):
                    for m, (a, b) in enumerate(((0, 0), (0, 1), (1, 0))):
                        last = pe.matmul(ps_y[tt // 2][:, tt % 2, :], hT[:, c % 2, a, tt * P:(tt + 1) * P], w2[:, b, c, :],
                                         start=(c == 0 and m == 0 and tt % 2 == 0), stop=(c == NC - 1 and m == 2 and tt % 2 == 1),
                                         skip_group_check=True)
                last.then_inc(yp, 1)

            def turn_x(i, j, r):
                pe.wait_ge(xnd, TB * i + 2 * r + 2)
                need(pe, xhi, ROUNDS * (i - 1) + r + 1, ROUNDS * (j - 1) + r + 1)
                need(pe, xlo, ROUNDS * (i - 1) + r + 1, ROUNDS * (j - 1) + r + 1)
                for tt in range(2):
                    for k in range(KT):
                        last = pe.transpose(ps_x[r][:, tt, k, :], xn[:, 2 * r + tt, k * P:(k + 1) * P], ident_sb[:, :])
                last.then_inc(xt, 1)

            def logits(i, j):
                pe.wait_ge(xhi, ROUNDS * (i + 1))
                pe.wait_ge(xlo, ROUNDS * (i + 1))
                need(pe, pne, i, j)
                split3(ps_r[0:NB, :], lambda a, k: rw[:, a, k, :], lambda b, k: turned(i, b, k), KT).then_inc(lgp, 1)

            def turn_logits(i, j):
                settle(pe, const, N_CONST)
                pe.wait_ge(lge, i + 1)
                need(pe, lgc, i, j)
                for tt in range(TB):
                    last = pe.transpose(ps_q[:, tt * NB:(tt + 1) * NB], lgT[:, tt * P:(tt + 1) * P], ident_sb[0:NB, 0:NB])
                last.then_inc(lgt, 1)

            def turn_penalties(i, j):
                pe.wait_ge(pnd, i + 1)
                for tt in range(TB):
                    last = pe.transpose(ps_pen[0:NB, tt * P:(tt + 1) * P], pen[:, tt, :], identb[:, :])
                last.then_inc(pnt, 1)

            pe.wait_ge(w_hi, N_SPLITS)
            pe.wait_ge(w_lo, N_SPLITS)
            pe.wait_ge(const, N_CONST)

            def body(t, t0):
                i, j = t - OFF["MM"], t0 - OFF["MM"]
                l, l0 = t - OFF["LN"], t0 - OFF["LN"]
                for c in range(NC):
                    if active("MM", t0):
                        first_product(i, j, c)
                    if c == 0:
                        if active("YT", t0):
                            second_product(t - OFF["YT"], t0 - OFF["YT"], NC - 1)
                    elif active("MM", t0):
                        second_product(i, j, c - 1)
                    if active("LN", t0):
                        if c == 2:
                            turn_x(l, l0, 0)
                        if c == 3:
                            turn_x(l, l0, 1)
                        if layer == 0 and c == 5:
                            logits(l, l0)
                        if layer == 0 and c == 6:
                            turn_logits(l, l0)
                        if layer == 0 and c == 7:
                            turn_penalties(l, l0)

            steps(pe, body)

        @block.scalar
        def _(act):
            act.wait_ge(w_in, 16 * N_LOADS)
            act.copy(w1[:, 0], w1raw[:, :, :]).then_inc(w_hi, 1)
            act.copy(w2[:, 0], w2raw[:, :, :]).then_inc(w_hi, 1)
            if layer == 0:
                act.copy(rw[:, 0], rwraw[:, :, :]).then_inc(w_hi, 1)

            def body(t, t0):
                i, j = t - OFF["MM"], t0 - OFF["MM"]
                l, l0 = t - OFF["LN"], t0 - OFF["LN"]
                for c in range(NC):
                    if active("MM", t0):
                        n, n0 = NC * i + c, NC * j + c
                        act.wait_ge(hp, n + 1)
                        need(act, hlo, n - 1, n0 - 1)
                        act.activation(h32[:, c % 2, :], ps_h[c % 2][:, :], ACT.Relu if layer == 0 else ACT.Gelu,
                                       bias=b1[:, c:c + 1]).then_inc(h32d, 1)
                        act.wait_ge(h32d, n + 1)
                        need(act, yp, n - 1, n0 - 1)
                        act.copy(hT[:, c % 2, 0, :], h32[:, c % 2, :]).then_inc(hhi, 1)
                    if active("LN", t0) and c in (3, 4):
                        r = c - 3
                        act.wait_ge(xt, ROUNDS * l + r + 1)
                        need(act, hp, NC * (l - 1), NC * (l0 - 1))
                        act.copy(xnT[:, bass.ds(parity(l) * 2 * KT, KT), 2 * r * P:(2 * r + 2) * P].rearrange("p k (t c) -> p t k c", t=2),
                                 ps_x[r][:, :, :, :]).then_inc(xhi, 1)
                    if active("LN", t0) and layer == 0 and c == 5:
                        act.wait_ge(lgp, l + 1)
                        need(act, lgt, l, l0)
                        act.activation(lgT[:, :], ps_r[0:NB, :], ACT.Identity, bias=rb[:, 0:1]).then_inc(lge, 1)
                    if active("LN", t0) and layer == 0 and c == 7:
                        act.wait_ge(pnt, l + 1)
                        act.copy(penT[0:NB, bass.ds(parity(l), 1), :].rearrange("p a s -> p (a s)"),
                                 ps_pen[0:NB, 0:S]).then_inc(pne, 1)

            steps(act, body)

        @block.vector
        def _(dve):
            dve.wait_ge(w_in, 16 * N_LOADS)
            dve.wait_ge(w_hi, 1)
            dve.tensor_tensor(w1[:, 1], w1raw[:, :, :], w1[:, 0].bitcast(F32), ALU.subtract).then_inc(w_lo, 1)
            dve.wait_ge(w_hi, 2)
            dve.tensor_tensor(w2[:, 1], w2raw[:, :, :], w2[:, 0].bitcast(F32), ALU.subtract).then_inc(w_lo, 1)
            if layer == 0:
                dve.wait_ge(w_hi, 3)
                dve.tensor_tensor(rw[:, 1], rwraw[:, :, :], rw[:, 0].bitcast(F32), ALU.subtract).then_inc(w_lo, 1)

            def body(t, t0):
                i, j = t - OFF["MM"], t0 - OFF["MM"]
                l, l0 = t - OFF["LN"], t0 - OFF["LN"]
                for c in range(NC):
                    if c == 0 and active("LN", t0):
                        for tt in range(TB):
                            need(dve, mvd, TB * l, TB * l0)
                            dve.bn_stats(stat[:, tt, :], x_sb[:, bass.ds(TB * l + tt, 1), :].rearrange("p a d -> p (a d)")).then_inc(bn, 1)
                        upto = in_register(dve, TB * (l + 1))
                        settle(dve, w_in, 16 * N_LOADS)
                        dve.wait_ge(bn, upto)
                        need(dve, xnd, TB * l, TB * l0)
                        need(dve, rsd, l, l0)
                        for tt in range(TB):
                            dve.bn_aggr(mv[:, tt, :], stat[:, tt, :]).then_inc(mvd, 1)
                    if c == 1:
                        if active("YT", t0):
                            y = t - OFF["YT"]
                            dve.wait_ge(yp, NC * (y + 1))
                            dve.wait_ge(xb, y + 1)
                            for r in range(ROUNDS):
                                xi = x_sb[:, bass.ds(TB * y + 2 * r, 2), :]
                                dve.tensor_tensor(xi, ps_y[r][:, :, :], xi, ALU.add).then_inc(yout, 1)
                        if active("LN", t0):
                            dve.wait_ge(rsd, l + 1)
                            need(dve, xt, ROUNDS * l, ROUNDS * l0)
                            for tt in range(TB):
                                dve.tensor_scalar(xn[:, tt, :], x_sb[:, bass.ds(TB * l + tt, 1), :].rearrange("p a d -> p (a d)"),
                                                  mv[:, tt, 0:1], rstd[:, 1, tt:tt + 1], ALU.subtract, ALU.mult).then_inc(xnd, 1)
                    if active("MM", t0):
                        n, n0 = NC * i + c, NC * j + c
                        dve.wait_ge(hhi, n + 1)
                        dve.tensor_tensor(hT[:, c % 2, 1, :], h32[:, c % 2, :], hT[:, c % 2, 0, :].bitcast(F32), ALU.subtract).then_inc(hlo, 1)
                    if active("LN", t0) and c in (3, 4):
                        r = c - 3
                        dve.wait_ge(xhi, ROUNDS * l + r + 1)
                        cols = slice(2 * r * P, (2 * r + 2) * P)
                        hi = xnT[:, bass.ds(parity(l) * 2 * KT, KT), cols]
                        lo = xnT[:, bass.ds(parity(l) * 2 * KT + KT, KT), cols]
                        for tt in range(2):
                            at = slice(tt * P, (tt + 1) * P)
                            ins_ = dve.tensor_tensor(lo[:, :, at], ps_x[r][:, tt, :, :], hi[:, :, at].bitcast(F32), ALU.subtract)
                        ins_.then_inc(xlo, 1)
                    if active("LN", t0) and layer == 0 and c == 6:
                        dve.wait_ge(lgt, l + 1)
                        need(dve, mrk, TB * l, TB * l0)
                        dve.tensor_copy(lg[:, :, :].rearrange("p t b -> p (t b)"), ps_q[:, 0:TB * NB]).then_inc(lgc, 1)
                        settle(dve, w_in, 16 * N_LOADS)
                        dve.wait_ge(lgc, l + 1)
                        for tt in range(TB):
                            dve.max(top8[:, tt, :], lg[:, tt, :]).then_inc(top, 1)
                        dve.wait_ge(top, TB * (l + 1))
                        dve.memset(top8[:, :, TOPK:8], -3.0e38).then_inc(abs8, 1)
                        settle(dve, w_in, 16 * N_LOADS)
                        dve.wait_ge(abs8, l + 1)
                        need(dve, pnd, l, l0)
                        for tt in range(TB):
                            dve.match_replace(marked[:, tt, :], top8[:, tt, :], lg[:, tt, :], 3.0e38).then_inc(mrk, 1)
                        dve.wait_ge(mrk, TB * (l + 1))
                        need(dve, pnt, l, l0)
                        dve.tensor_scalar(pen[:, :, :], marked[:, :, :], 3.0e38, -BLOCK_BIG, ALU.is_lt, ALU.mult).then_inc(pnd, 1)

            steps(dve, body)

        @block.gpsimd
        def _(pool):
            pool.memset(half[:, :], -0.5).then_inc(const, 1)
            if layer == 0:
                pool.memset(identb[:, :], 0.0).then_inc(const, 1)
                pool.memset(spread[:, :], 1.0).then_inc(const, 1)
                pool.memset(penT[:, :, :].rearrange("p a s -> p (a s)"), 0.0).then_inc(const, 1)
                pool.wait_ge(const, 3)
                pool.affine_select(out=identb[:, :], in_=identb[:, :], compare_op=ALU.not_equal, fill=1.0,
                                   base=0, pattern=[[-1, P]], channel_multiplier=1).then_inc(const, 1)
                width = FF // NB
                pool.affine_select(out=spread[:, :], in_=spread[:, :], compare_op=ALU.is_ge, fill=0.0,
                                   base=0, pattern=[[1, FF]], channel_multiplier=-width).then_inc(const, 1)
                pool.wait_ge(const, 6)
                pool.affine_select(out=spread[:, :], in_=spread[:, :], compare_op=ALU.is_ge, fill=0.0,
                                   base=width - 1, pattern=[[-1, FF]], channel_multiplier=width).then_inc(const, 1)
            pool.wait_ge(const, N_CONST)
            pool.wait_ge(w_in, 16 * N_LOADS)

            def body(t, t0):
                l, l0 = t - OFF["LN"], t0 - OFF["LN"]
                if active("LN", t0):
                    upto, before = in_register(pool, TB * (l + 1)), in_register(pool, TB * l)
                    settle(pool, w_in, 16 * N_LOADS)
                    pool.wait_ge(mvd, upto)
                    need(pool, xnd, before, TB * l0)
                    pool.tensor_scalar(rstd[:, 0, :], mv[:, :, 1], EPS, None, ALU.add).then_inc(var1, 1)
                    pool.wait_ge(var1, l + 1)
                    pool.tensor_tensor(rstd[:, 1, :], rstd[:, 0, :], half[:, :], ALU.pow).then_inc(rsd, 1)
                    pool.wait_ge(xnd, TB * (l + 1))
                    xi = x_sb[:, bass.ds(TB * l, TB), :]
                    pool.tensor_tensor(xi, xi, b2_b[:, :, :].to_broadcast([P, TB, D]), ALU.add).then_inc(xb, 1)

            steps(pool, body)


def build(nc, x, ctxT, maskT, wq0, bq0, wk0, bk0, wv0, bv0, wo0, bo0, rw, rb, w1a, b1a, w2a, b2a,
          wq1, bq1, wk1, bk1, wv1, bv1, wo1, bo1, w1b, b1b, w2b, b2b, out):
    B, S, D = x.shape
    NT = B * S // P
    scratch = nc.dram_tensor("scratch", (2, 2, P, S), F16).ap()
    scratch_w = nc.dram_tensor("scratch_w", (4, P, 4 * P), F32).ap()
    with ExitStack() as ctx:
        x_sb = ctx.enter_context(nc.sbuf_tensor("x_sb", [P, NT, D], F32))
        ident_sb = ctx.enter_context(nc.sbuf_tensor("ident_sb", [P, P], F32))
        stack = ctx.enter_context(nc.sbuf_tensor("stack", [P, 2 * 4 * 8, S], F16))
        xt = x.rearrange("b (t p) d -> p (b t) d", p=P)
        outt = out.rearrange("b (t p) d -> p (b t) d", p=P)
        attention_phase(nc, 0, x_sb, ident_sb, stack,
                        dict(x=xt, ctxT=ctxT, maskT=maskT, wqT=wq0, bq=bq0, wkT=wk0, bk=bk0, wvT=wv0, bv=bv0, woT=wo0, bo=bo0),
                        scratch, scratch_w, B, S, D)
        ffn_phase(nc, 0, x_sb, ident_sb, dict(rw=rw, rb=rb, w1=w1a, b1=b1a, w2=w2a, b2=b2a), None, B, S, D, w1a.shape[1])
        attention_phase(nc, 1, x_sb, ident_sb, stack,
                        dict(ctxT=ctxT, wqT=wq1, bq=bq1, wkT=wk1, bk=bk1, wvT=wv1, bv=bv1, woT=wo1, bo=bo1),
                        scratch, scratch_w, B, S, D)
        ffn_phase(nc, 1, x_sb, ident_sb, dict(w1=w1b, b1=b1b, w2=w2b, b2=b2b), outt, B, S, D, w1b.shape[1])


_LAYOUT = [
    ("x", None), ("ctx_1024", "tokens"), ("mask_1x1xSxS2_if1", "mask"),
    ("L0_xattn_w_Q", "T"), ("L0_xattn_b_Q", None), ("L0_xattn_w_K", "T"), ("L0_xattn_b_K", None),
    ("L0_xattn_w_V", "T"), ("L0_xattn_b_V", None), ("L0_xattn_w_O", "T"), ("L0_xattn_b_O", None),
    ("L0_ffn_router_w", "T"), ("L0_ffn_router_b", None), ("L0_ffn_w1", "T"), ("L0_ffn_b1", None),
    ("L0_ffn_w2", "T"), ("L0_ffn_b2", None),
    ("L1_xattn_wq_w", "T"), ("L1_xattn_wq_b", None), ("L1_xattn_wk_w", "T"), ("L1_xattn_wk_b", None),
    ("L1_xattn_wv_w", "T"), ("L1_xattn_wv_b", None), ("L1_xattn_wo_w", "T"), ("L1_xattn_wo_b", None),
    ("L1_ffn_w1", None), ("L1_ffn_b1", None), ("L1_ffn_w2", None), ("L1_ffn_b2", None),
]


def kernel(**inputs):
    import numpy as _np
    import concourse.bacc as _bacc
    from concourse import mybir as _mybir
    from concourse.bass_utils import run_bass_kernel_spmd as _run

    nc = _bacc.Bacc("TRN2", target_bir_lowering=False, num_devices=1)
    arrays, args = {}, []
    for name, how in _LAYOUT:
        a = _np.asarray(inputs[name])
        if how == "tokens":
            a = a.reshape(-1, a.shape[-1])
        if how == "mask":
            a = a.reshape(a.shape[-2], a.shape[-1])
        if how is not None:
            a = a.T
        a = _np.ascontiguousarray(a)
        arrays[f"in_{name}"] = a
        args.append(nc.dram_tensor(f"in_{name}", a.shape, _mybir.dt.from_np(a.dtype), kind="ExternalInput").ap())
    shape = inputs["x"].shape
    args.append(nc.dram_tensor("out_0", shape, _mybir.dt.float32, kind="ExternalOutput").ap())
    build(nc, *args)
    r = _run(nc, [arrays], core_ids=[0])
    return r.results[0]["out_0"]
```

```python
from contextlib import ExitStack

import concourse.bass as bass
from concourse import mybir

P = 128
F32 = mybir.dt.float32
FR = mybir.dt.float32r
F16 = mybir.dt.float16
BF16 = mybir.dt.bfloat16
I32 = mybir.dt.int32
ALU = mybir.AluOpType
ACT = mybir.ActivationFunctionType
AX_X = mybir.AxisListType.X

H = 16
DH = 16
G = 4
EPS = 1e-5
MASK_BIG = float(2**19)
MAX_SCALE = 16.0
SCORE_ROWS = 112
MAX_ROW = SCORE_ROWS
MAX_SCALE_TWICE = 33632256.0
BLOCK_BIG = 1e30


UNROLL = 4


def need(eng, sem, value, least):
    if least > 0:
        eng.wait_ge(sem, value)


def in_register(eng, value):
    return value if isinstance(value, int) else eng.to_reg(value)


def held(eng, value, most):
    return value if isinstance(value, int) else eng.snap(eng.to_reg(value), donate=True, min_val=0, max_val=most)


def settle(eng, sem, value):
    eng.wait_ge(sem, value)


def stage_steps(n_steps, offsets):
    last = max(offsets) + n_steps
    ramp = max(offsets) + 2
    cuts = sorted({o + n_steps for o in offsets} | {last})
    ranges = [(t, t + 1) for t in range(ramp)]
    at = ramp
    for c in cuts:
        odd = (c - at) % UNROLL if c - at >= 2 * UNROLL else max(c - at, 0)
        ranges += [(t, t + 1) for t in range(at, at + odd)]
        if c > at + odd:
            ranges.append((at + odd, c))
        at = max(at, c)
    return ranges


def attention_phase(nc, layer, x_sb, ident_sb, stack, ins, scratch, scratch_w, B, S, D):
    NT = B * S // P
    TB = S // P
    KT = D // P
    EXP_TILES = [(0, 1), (2,), (3,)]
    VW = 2 * DH + 1
    OFF = dict(LD=0, LN=1, PW=4, PR=5, VW=7, VP=8, SM=10, MR=11, PV=12, TL=13, OT=16, OP=17)
    RANGES = stage_steps(NT, list(OFF.values()))

    def active(name, t0):
        return OFF[name] <= t0 < OFF[name] + NT

    with ExitStack() as ctx:
        ctx.enter_context(nc.cleanup_on_exit())

        def sb(name, shape, dt):
            return ctx.enter_context(nc.sbuf_tensor(f"L{layer}a_{name}", shape, dt))

        def sem(name):
            return nc.alloc_semaphore(name=f"L{layer}a_{name}")

        src = sb("src", [P, 2 * 2 * 2 * KT, S], FR)
        wv = sb("wv", [P, 2, KT, D], FR)
        wo = sb("wo", [P, 2, KT, D], FR)
        wqk_now = sb("wqk_now", [P, 2, 2 * KT, P], FR)
        vsrc = sb("vsrc", [P, 2, 2 * KT, P], FR)
        osrc = sb("osrc", [P, 2, D], F32)
        probs = sb("probs", [P, 2, TB, S], F32)
        plo = sb("plo", [P, 2, TB, S], F16)
        v16 = sb("v16", [P, 2 * TB * H, VW], F16)
        o_sb = sb("o_sb", [P, 2 * TB, D], F32)
        o_raw = sb("o_raw", [P, 2, TB, VW], F32)
        o_sum = sb("o_sum", [P, 2, TB, DH], F32)
        o_rec = sb("o_rec", [P, 2, TB], F32)
        oT = sb("oT", [P, 2, KT, P], FR)
        q32 = sb("q32", [P, S], F32)
        qhl = sb("qhl", [P, 2, S], F16)
        v32 = sb("v32", [P, D], F32)
        craw = sb("craw", [P, 2, KT, P], F32)
        xn = sb("xn", [P, D], F32)
        stat = sb("stat", [P, 6], F32)
        mv = sb("mv", [P, 2], F32)
        rstd = sb("rstd", [P, 3], F32)
        half = sb("half", [P, 1], F32)
        maskT, keep = None, None
        if layer == 0:
            maskT = sb("maskT", [P, TB, S], BF16)
            keep = o_sb[:, :, :].bitcast(BF16).rearrange("p a d -> p (a d)").rearrange("p (a s) -> p a s", s=S)[:, 0:TB, :]
            mraw = plo[:, :, :, :].rearrange("p a b s -> p (a b s)").bitcast(I32).rearrange("p (a s) -> p a s", a=TB)
            kept = sb("kept", [P, 1], F32)
            kept_all = sb("kept_all", [1, 1], I32)
            onesb = sb("onesb", [P, P], BF16)
            onesf = sb("onesf", [P, P], F32)
        nmax = sb("nmax", [P, 2, G * TB], BF16)
        mrow = sb("mrow", [G * TB, P], F16)
        identb = sb("identb", [P, P], BF16)
        bqk = sb("bqk", [P, 4], F32)
        bv_b = sb("bv_b", [P, D], F32)
        bo_b = sb("bo_b", [P, D], F32)
        rowany = sb("rowany", [P, 2, S], BF16)

        ps_t = ctx.enter_context(nc.psum_tensor(f"L{layer}a_ps_t", [P, 2, S], F32))
        ps_u = ctx.enter_context(nc.psum_tensor(f"L{layer}a_ps_u", [P, S], F32))
        ps_s = [ctx.enter_context(nc.psum_tensor(f"L{layer}a_ps_s{c}", [P, S], F32)) for c in range(2)]
        ps_o = ctx.enter_context(nc.psum_tensor(f"L{layer}a_ps_o", [P, 512], F32))
        ps_m = ctx.enter_context(nc.psum_tensor(f"L{layer}a_ps_m", [P, 512], F32))
        ps_n = ctx.enter_context(nc.psum_tensor(f"L{layer}a_ps_n", [P, 512], F32))

        w_in, b_in = sem("w_in"), sem("b_in")
        w_st = sem("w_st")
        w_hi, w_lo = sem("w_hi"), sem("w_lo")
        x_in, c_in = sem("x_in"), sem("c_in")
        bn, mvd, var1, pwd, rsd, xnd = sem("bn"), sem("mvd"), sem("var1"), sem("pwd"), sem("rsd"), sem("xnd")
        xt, xhi, xlo = sem("xt"), sem("xhi"), sem("xlo")
        chi, clo = sem("chi"), sem("clo")
        xb = sem("xb")
        wnow, vnow, onow = sem("wnow"), sem("vnow"), sem("onow")
        prj, q32d, qhi, qlo = sem("prj"), sem("q32d"), sem("qhi"), sem("qlo")
        scr_w, stk = sem("scr_w"), sem("stk")
        vprj, v32d, vhi, vlo = sem("vprj"), sem("v32d"), sem("vhi"), sem("vlo")
        scq, smax = sem("scq"), sem("smax")
        mtr, mev, mdm = sem("mtr"), sem("mev"), sem("mdm")
        sck, pexp = sem("sck"), sem("pexp")
        plo_v, plo_g = sem("plo_v"), sem("plo_g")
        pv, oev, orc, oad, onm = sem("pv"), sem("oev"), sem("orc"), sem("oad"), sem("onm")
        otr, ohi, olo, oprj, xout = sem("otr"), sem("ohi"), sem("olo"), sem("oprj"), sem("xout")
        setup_g, setup_v, setup_w, setup_p = sem("setup_g"), sem("setup_v"), sem("setup_w"), sem("setup_p")
        N_LOADS = 7 if layer == 0 else 6
        N_BIASES = 4
        G_FIRST = 5 if layer == 0 else 3
        G_SETUP = 9 if layer == 0 else 4
        WEIGHTS_AT = OFF["PW"]
        V_SETUP = 9 if layer == 0 else 1

        wraw = probs[:, :, :, :].rearrange("p a b s -> p (a b s)")
        wraw_qk = wraw[:, 0:4 * KT * P].rearrange("p (m k c) -> p m k c", m=4, k=KT)
        wraw_v = wraw[:, 1024:1024 + KT * D].rearrange("p (k c) -> p k c", k=KT)
        wraw_o = wraw[:, 1536:1536 + KT * D].rearrange("p (k c) -> p k c", k=KT)
        wqk_v = wraw[:, 2048:4096].bitcast(FR).rearrange("p (m h k c) -> p m h k c", m=4, h=2, k=KT)

        ctxT = ins["ctxT"].rearrange("(k p) t -> p k t", p=P)
        scr = scratch.rearrange("a h (j d) s -> (a h) d j s", d=DH)
        scr_out = scratch.rearrange("a h p s -> a p h s")

        USES = dict(m=["OP", "PR", "OT"], n=["MR", "VP", "LN"])

        def users(bank, t0):
            return [u for u in USES[bank] if active(u, t0)]

        def masked_rows(t0):
            return layer == 0 and (t0 - OFF["PR"]) % 2 == 0

        read_out = dict(MR=mev, PR=q32d, VP=v32d, LN=xlo, OT=olo, OP=xout)

        def steps(eng, body, first=0, end=RANGES[-1][1]):
            for t0, t1 in RANGES:
                if not first <= t0 < end:
                    continue
                if t1 - t0 == 1:
                    body(t0, t0)
                else:
                    with eng.Fori(t0, t1 - UNROLL + 1, UNROLL) as t:
                        for more in range(UNROLL):
                            body(t + more, t0 + more)

        def parity(i):
            return (i // TB) % 2

        def batch_end(i):
            return TB * (i // TB) + TB

        def prior_batch(i):
            return TB * ((i - TB) // TB)

        block = ctx.enter_context(nc.Block())

        @block.sync
        def _(sp):
            sp.dma_start(bqk[:, 0:4:2], ins["bq"].rearrange("(m p) -> p m", p=P),
                         allow_slow_non_contiguous=True).then_inc(b_in, 16)
            sp.dma_start(bqk[:, 1:4:2], ins["bk"].rearrange("(m p) -> p m", p=P),
                         allow_slow_non_contiguous=True).then_inc(b_in, 16)
            sp.dma_start(bv_b[:, :], ins["bv"].partition_broadcast(P)).then_inc(b_in, 16)
            sp.dma_start(bo_b[:, :], ins["bo"].partition_broadcast(P)).then_inc(b_in, 16)

            def body(t, t0):
                i, j = t - OFF["PW"], t0 - OFF["PW"]
                if active("PW", t0):
                    before, done = in_register(sp, i - 1), in_register(sp, 16 * i)
                    settle(sp, w_st, 16)
                    need(sp, wnow, done, 16 * j)
                    need(sp, prj, before, j - 1)
                    sp.dma_start(wqk_now[:, bass.ds(j % 2, 1)].rearrange("p a k c -> p (a k c)").bitcast(F32),
                                 scratch_w[bass.ds(j % 4, 1)].rearrange("m p c -> (m p) c")).then_inc(wnow, 16)
                i, j = t - OFF["VW"], t0 - OFF["VW"]
                if active("VW", t0):
                    before, done, upto = in_register(sp, i - 1), in_register(sp, 16 * i), in_register(sp, i + 1)
                    settle(sp, w_st, 16)
                    need(sp, vnow, done, 16 * j)
                    need(sp, vprj, before, j - 1)
                    sp.wait_ge(chi, upto)
                    sp.wait_ge(clo, upto)
                    sp.dma_start(vsrc[:, bass.ds(j % 2, 1)].rearrange("p a k c -> p (a k) c").bitcast(F32),
                                 src[:, bass.ds(parity(i) * 8 + 4, 2 * KT), bass.ds((j % TB) * P, P)].bitcast(F32)).then_inc(vnow, 16)
                i, j = t - OFF["LD"], t0 - OFF["LD"]
                if active("LD", t0):
                    before, done = in_register(sp, i - 1), in_register(sp, 16 * i)
                    settle(sp, setup_g, 1)
                    need(sp, clo, before, j - 1)
                    need(sp, c_in, done, 16 * j)
                    if layer == 0:
                        need(sp, x_in, done, 16 * j)
                        sp.dma_start(x_sb[:, bass.ds(i, 1), :], ins["x"][:, bass.ds(i, 1), :]).then_inc(x_in, 16)
                    sp.dma_start(craw[:, bass.ds(j % 2, 1)], ctxT[:, :, bass.ds(i * P, P)]).then_inc(c_in, 16)
                i, j = t - OFF["MR"], t0 - OFF["MR"]
                if active("MR", t0):
                    sp.wait_ge(mev, i + 1)
                    heads = parity(i) * 32 + ((j % 4) // 2) * 16 + (j % 2) * G
                    sp.dma_start(
                        stack[MAX_ROW:MAX_ROW + 1, bass.ds(heads, G), :].rearrange("o h (t q) -> o (h t) q", q=P),
                        mrow[:, :]).then_inc(mdm, 16)
                i, j = t - OFF["OT"], t0 - OFF["OT"]
                if active("OT", t0):
                    before, done, heads = in_register(sp, i - 1), in_register(sp, 16 * i), in_register(sp, G * batch_end(i))
                    settle(sp, w_st, 16)
                    need(sp, otr, before, j - 1)
                    need(sp, onow, done, 16 * j)
                    sp.wait_ge(onm, heads)
                    sp.dma_start(osrc[:, j % 2, :], o_sb[:, bass.ds(parity(i) * TB + j % TB, 1), :].rearrange("p a d -> p (a d)")).then_inc(onow, 16)
                i, j = t - OFF["PR"], t0 - OFF["PR"]
                if active("PR", t0):
                    stacked, upto = in_register(sp, 48 * i), in_register(sp, i + 1)
                    settle(sp, w_st, 16)
                    need(sp, stk, stacked, 48 * j)
                    sp.wait_ge(qhi, upto)
                    sp.wait_ge(qlo, upto)
                    sp.dma_start(scr_out[bass.ds(j % 2, 1)].rearrange("a p h s -> (a p) h s"), qhl[:, :, :]).then_inc(scr_w, 16)
                    scored = in_register(sp, 12 * (4 * ((i - 8) // 4) + 2 * ((j % 4) // 2) + 2))
                    written = in_register(sp, 16 * (i + 1))
                    settle(sp, w_st, 16)
                    need(sp, sck, scored, 12 * (4 * ((j - 8) // 4) + 2 * ((j % 4) // 2) + 2))
                    sp.wait_ge(scr_w, written)
                    dst = bass.ds(8 * (4 * parity(i) + j % 4), 8)
                    is_k = j % 2
                    for r, half_no in enumerate([0, is_k, 1 - is_k]):
                        sp.dma_start(stack[r * DH:(r + 1) * DH, dst, :],
                                     scr[bass.ds(2 * (j % 2) + half_no, 1)].rearrange("a d j s -> (a d) j s")).then_inc(stk, 16)

            steps(sp, body, 0, 1)
            if layer == 0:
                sp.dma_start(mraw, ins["maskT"].rearrange("(k p) q -> p k q", p=P)).then_inc(w_in, 16)
            for m in range(4):
                w = ins["wqT" if m % 2 == 0 else "wkT"].rearrange("(k p) c -> p k c", p=P)
                sp.dma_start(wraw_qk[:, m], w[:, :, (m // 2) * P:(m // 2 + 1) * P]).then_inc(w_in, 16)
            sp.dma_start(wraw_v, ins["wvT"].rearrange("(k p) c -> p k c", p=P)).then_inc(w_in, 16)
            sp.dma_start(wraw_o, ins["woT"].rearrange("(k p) c -> p k c", p=P)).then_inc(w_in, 16)
            steps(sp, body, 1, WEIGHTS_AT)
            sp.wait_ge(w_hi, 1)
            sp.wait_ge(w_lo, 1)
            sp.dma_start(scratch_w.rearrange("m p c -> p m c"), wqk_v.rearrange("p m h k c -> p m (h k c)").bitcast(F32)).then_inc(w_st, 16)
            sp.wait_ge(w_st, 16)
            steps(sp, body, WEIGHTS_AT)
            sp.wait_ge(scr_w, 16 * NT)
            sp.wait_ge(stk, 48 * NT)

        @block.tensor
        def _(pe):
            def split3(out, lhs, rhs, n):
                pairs = [(a, b, k) for a, b in ((0, 0), (0, 1), (1, 0)) for k in range(n)]
                for m, (a, b, k) in enumerate(pairs):
                    last = pe.matmul(out, lhs(a, k), rhs(b, k), start=(m == 0), stop=(m == len(pairs) - 1))
                return last

            def build(masked):
                def one_score(out, rows, a, b, at, mask_parts):
                    last = pe.matmul(out, stack[0:rows, bass.ds(a, 1), at * P:(at + 1) * P].rearrange("p a s -> p (a s)"),
                                     stack[0:rows, bass.ds(b, 1), :].rearrange("p a s -> p (a s)"),
                                     start=True, stop=not masked)
                    if masked:
                        for m, (o, lhs, rhs) in enumerate(mask_parts):
                            last = pe.matmul(o, lhs, rhs, start=False, stop=(m == len(mask_parts) - 1))
                    return last

                def first_q_head(i, j):
                    return held(pe, parity(i) * 32 + ((j % 4) // 2) * 16 + (j % 2) * G, 2 * 32 - 8 - G)

                def scores_q(t, t0, hh, tiles, head):
                    i, j = t - OFF["SM"], t0 - OFF["SM"]
                    if not active("SM", t0):
                        return
                    if hh == 0 and tiles[0] == 0:
                        pe.wait_ge(stk, 48 * batch_end(i))
                    for qt in tiles:
                        n, n0 = 16 * i + 4 * hh + qt, 16 * j + 4 * hh + qt
                        need(pe, smax, n - 1, n0 - 1)
                        out = ps_s[qt % 2]
                        parts = [(out[:, kt * P:(kt + 1) * P], maskT[:, kt, qt * P:(qt + 1) * P], identb[:, :])
                                 for kt in range(TB)] if masked else []
                        one_score(out[:, :], SCORE_ROWS, head + hh, head + hh + 8, qt, parts).then_inc(scq, 1)

                def scores_k(t, t0, hh, c, head):
                    i, j = t - OFF["PV"], t0 - OFF["PV"]
                    if not active("PV", t0):
                        return
                    if hh == 0 and c == 0:
                        pe.wait_ge(mdm, 16 * (i + 1))
                    m, m0 = G * i + hh, G * j + hh
                    back = 2 if c == 0 else 0 if c == 1 else -2
                    need(pe, pexp, 3 * m - back, 3 * m0 - back)
                    for kt in EXP_TILES[c]:
                        out = ps_t[:, kt, :] if c == 0 else ps_u[:, :]
                        parts = [(out, identb[:, :], maskT[:, kt, :])] if masked else []
                        last = one_score(out, MAX_ROW + 1, head + hh + 8, head + hh, kt, parts)
                    last.then_inc(sck, 1)

                def times_v(i, j, hh):
                    m, m0 = G * i + hh, G * j + hh
                    v_first = held(pe, parity(i) * TB * H + (j % 4) * G + hh, TB * H + 3 * G + 3)
                    pe.wait_ge(plo_v, m + 1)
                    pe.wait_ge(plo_g, m + 1)
                    need(pe, oev, m, m0)
                    if hh == 0:
                        pe.wait_ge(vhi, batch_end(i))
                        pe.wait_ge(vlo, batch_end(i))
                    hi = probs[:, hh % 2, :, :].bitcast(BF16)
                    for qt in range(TB):
                        for kt in range(TB):
                            for part in range(2):
                                if part == 0:
                                    lhs = hi[:, kt, 2 * qt * P + 1:2 * (qt + 1) * P:2]
                                else:
                                    lhs = plo[:, hh % 2, kt, qt * P:(qt + 1) * P]
                                last = pe.matmul(ps_o[:, qt * VW:(qt + 1) * VW], lhs,
                                                 v16[:, bass.ds(v_first + kt * H, 1), :].rearrange("p a w -> p (a w)"),
                                                 start=(kt == 0 and part == 0), stop=(kt == TB - 1 and part == 1))
                    last.then_inc(pv, 1)

                def shared(name, t, t0):
                    bank = "m" if name in USES["m"] else "n"
                    at = users(bank, t0).index(name)
                    if at > 0:
                        before = users(bank, t0)[at - 1]
                        pe.wait_ge(read_out[before], t - OFF[before] + 1)
                        return
                    earlier = [r for r in RANGES if r[1] <= t0 and users(bank, r[0])]
                    if earlier and t0 in [r[0] for r in RANGES]:
                        before = users(bank, earlier[-1][0])[-1]
                        pe.wait_ge(read_out[before], earlier[-1][1] - OFF[before])
                    if not isinstance(t, int):
                        before = users(bank, t0)[-1]
                        if t0 > OFF[before]:
                            pe.wait_ge(read_out[before], t - OFF[before])

                def max_rows(t, t0):
                    if active("MR", t0):
                        i, j = t - OFF["MR"], t0 - OFF["MR"]
                        pe.wait_ge(smax, 16 * (i + 1))
                        shared("MR", t, t0)
                        pe.matmul(ps_n[0:G * TB, 0:P], nmax[:, bass.ds(j % 2, 1), :].rearrange("p a c -> p (a c)"),
                                  identb[:, :], start=True, stop=True).then_inc(mtr, 1)

                def project(t, t0):
                    if active("PR", t0):
                        i, j = t - OFF["PR"], t0 - OFF["PR"]
                        base = held(pe, parity(i) * 8 + 4 * (j % 2), 12)
                        split = in_register(pe, batch_end(i))
                        for s in (xhi, xlo, chi, clo):
                            pe.wait_ge(s, split)
                        pe.wait_ge(wnow, 16 * (i + 1))
                        shared("PR", t, t0)
                        split3(ps_m[:, :], lambda a, k: wqk_now[:, j % 2, a * KT + k, :],
                               lambda b, k: src[:, bass.ds(base + b * KT + k, 1), :].rearrange("p a s -> p (a s)"), KT).then_inc(prj, 1)

                def project_v(t, t0):
                    if active("VP", t0):
                        i, j = t - OFF["VP"], t0 - OFF["VP"]
                        pe.wait_ge(vnow, 16 * (i + 1))
                        shared("VP", t, t0)
                        split3(ps_n[:, 0:D], lambda a, k: vsrc[:, j % 2, a * KT + k, :], lambda b, k: wv[:, b, k, :], KT).then_inc(vprj, 1)

                def turn_x(t, t0):
                    if active("LN", t0):
                        i, j = t - OFF["LN"], t0 - OFF["LN"]
                        pe.wait_ge(xnd, i + 1)
                        shared("LN", t, t0)
                        for k in range(KT):
                            last = pe.transpose(ps_n[:, k * P:(k + 1) * P], xn[:, k * P:(k + 1) * P], ident_sb[:, :])
                        last.then_inc(xt, 1)

                def turn_o(t, t0):
                    if active("OT", t0):
                        i, j = t - OFF["OT"], t0 - OFF["OT"]
                        pe.wait_ge(onow, 16 * (i + 1))
                        shared("OT", t, t0)
                        for k in range(KT):
                            last = pe.transpose(ps_m[:, k * P:(k + 1) * P], osrc[:, j % 2, k * P:(k + 1) * P], ident_sb[:, :])
                        last.then_inc(otr, 1)

                def project_o(t, t0):
                    if active("OP", t0):
                        i, j = t - OFF["OP"], t0 - OFF["OP"]
                        pe.wait_ge(ohi, i + 1)
                        pe.wait_ge(olo, i + 1)
                        shared("OP", t, t0)
                        split3(ps_m[:, 0:D], lambda a, k: oT[:, a, k, :], lambda b, k: wo[:, b, k, :], KT).then_inc(oprj, 1)

                def body(t, t0):
                    head_q = first_q_head(t - OFF["SM"], t0 - OFF["SM"]) if active("SM", t0) else None
                    head_k = first_q_head(t - OFF["PV"], t0 - OFF["PV"]) if active("PV", t0) else None
                    for hh in range(G):
                        scores_k(t, t0, hh, 0, head_k)
                        scores_q(t, t0, hh, (0, 1), head_q)
                        if hh == 0:
                            project_o(t, t0)
                        if hh == 1:
                            project(t, t0)
                        if hh == 2:
                            project_v(t, t0)
                        if hh == 3:
                            turn_o(t, t0)
                            turn_x(t, t0)
                        scores_k(t, t0, hh, 1, head_k)
                        scores_q(t, t0, hh, (2, 3), head_q)
                        scores_k(t, t0, hh, 2, head_k)
                        if hh == 0:
                            max_rows(t, t0)
                        if hh > 0 and active("PV", t0):
                            times_v(t - OFF["PV"], t0 - OFF["PV"], hh - 1)
                        if hh == 0 and active("TL", t0):
                            times_v(t - OFF["TL"], t0 - OFF["TL"], G - 1)

                return body

            pe.wait_ge(setup_g, G_FIRST)
            steps(pe, build(False), 0, WEIGHTS_AT)
            if layer == 0:
                pe.wait_ge(setup_v, 1)
                pe.wait_ge(setup_g, G_FIRST + 2)
                for kt in range(TB):
                    last = pe.matmul(ps_m[:, :], onesb[:, :], keep[:, kt, :], start=(kt == 0), stop=(kt == TB - 1))
                last.then_inc(setup_p, 1)
                pe.wait_ge(setup_v, 2)
                pe.matmul(ps_o[:, 0:1], onesf[:, :], kept[:, :], start=True, stop=True).then_inc(setup_p, 1)
                pe.wait_ge(setup_v, V_SETUP)
                pe.wait_ge(setup_g, G_SETUP)
                kept_count = pe.value_load(kept_all[0:1, 0:1], min_val=0, max_val=S * S)
                with pe.If(kept_count < S * S):
                    steps(pe, build(True), WEIGHTS_AT)
                with pe.Else():
                    steps(pe, build(False), WEIGHTS_AT)
            else:
                pe.wait_ge(setup_g, G_SETUP)
                pe.wait_ge(setup_v, V_SETUP)
                steps(pe, build(False), WEIGHTS_AT)

        @block.scalar
        def _(act):
            def exponentials(t, t0, hh, c):
                i, j = t - OFF["PV"], t0 - OFF["PV"]
                if active("PV", t0):
                    m, m0 = G * i + hh, G * j + hh
                    act.wait_ge(sck, 3 * m + c + 1)
                    need(act, pv, m - 1, m0 - 1)
                    tiles = EXP_TILES[c]
                    act.activation(probs[:, hh % 2, tiles[0]:tiles[-1] + 1, :].rearrange("p a s -> p (a s)"),
                                   ps_t[:, :, :].rearrange("p a s -> p (a s)") if c == 0 else ps_u[:, :], ACT.Exp,
                                   scale=1.0 / DH**0.5).then_inc(pexp, 1)

            def take_o(i, j, hh):
                m, m0 = G * i + hh, G * j + hh
                act.wait_ge(pv, m + 1)
                need(act, onm, m - 1, m0 - 1)
                act.copy(o_raw[:, hh % 2, :, :], ps_o[:, 0:TB * VW].rearrange("p (a w) -> p a w", a=TB)).then_inc(oev, 1)

            def body(t, t0):
                for hh in range(G):
                    if hh < 2:
                        if active("TL", t0):
                            take_o(t - OFF["TL"], t0 - OFF["TL"], hh + 2)
                    elif active("PV", t0):
                        take_o(t - OFF["PV"], t0 - OFF["PV"], hh - 2)
                    exponentials(t, t0, hh, 0)
                    if hh == 2 and active("PR", t0) and not masked_rows(t0):
                        i, j = t - OFF["PR"], t0 - OFF["PR"]
                        act.wait_ge(prj, i + 1)
                        need(act, qhi, i, j)
                        need(act, qlo, i, j)
                        act.activation(q32[:, :], ps_m[:, :], ACT.Identity, bias=bqk[:, j % 4:j % 4 + 1]).then_inc(q32d, 1)
                    if hh == 0 and active("LN", t0):
                        i, j = t - OFF["LN"], t0 - OFF["LN"]
                        act.wait_ge(c_in, 16 * (i + 1))
                        need(act, prj, prior_batch(i), prior_batch(j))
                        need(act, vnow, 16 * (i - 7), 16 * (j - 7))
                        at = parity(i) * 8 + 4
                        act.copy(src[:, bass.ds(at, KT), bass.ds((j % TB) * P, P)], craw[:, bass.ds(j % 2, 1)].rearrange("p a k c -> p (a k) c")).then_inc(chi, 1)
                    exponentials(t, t0, hh, 1)
                    if hh == 2 and active("LN", t0):
                        i, j = t - OFF["LN"], t0 - OFF["LN"]
                        act.wait_ge(rsd, i + 1)
                        need(act, xt, i, j)
                        act.activation(xn[:, :], x_sb[:, bass.ds(i, 1), :].rearrange("p a d -> p (a d)"), ACT.Identity,
                                       scale=rstd[:, 1:2], bias=rstd[:, 2:3]).then_inc(xnd, 1)
                    exponentials(t, t0, hh, 2)
                    if hh == 2 and active("PR", t0):
                        i, j = t - OFF["PR"], t0 - OFF["PR"]
                        act.wait_ge(q32d, i + 1)
                        need(act, scr_w, 16 * i, 16 * j)
                        act.copy(qhl[:, 0, :], q32[:, :]).then_inc(qhi, 1)
                    if hh == 3 and active("OT", t0):
                        i, j = t - OFF["OT"], t0 - OFF["OT"]
                        act.wait_ge(otr, i + 1)
                        need(act, oprj, i, j)
                        act.copy(oT[:, 0], ps_m[:, 0:D].rearrange("p (k c) -> p k c", k=KT)).then_inc(ohi, 1)
                    if hh == 3 and active("LN", t0):
                        i, j = t - OFF["LN"], t0 - OFF["LN"]
                        act.wait_ge(xt, i + 1)
                        need(act, prj, prior_batch(i), prior_batch(j))
                        act.copy(src[:, bass.ds(parity(i) * 8, KT), bass.ds((j % TB) * P, P)],
                                 ps_n[:, 0:D].rearrange("p (k c) -> p k c", k=KT)).then_inc(xhi, 1)
                    if hh == 3 and active("VP", t0):
                        i, j = t - OFF["VP"], t0 - OFF["VP"]
                        act.wait_ge(v32d, i + 1)
                        need(act, pv, 4 * G * ((i - TB) // TB), 4 * G * ((j - TB) // TB))
                        act.copy(v16[:, bass.ds(parity(i) * TB * H + (j % TB) * H, H), 0:DH],
                                 v32[:, :].rearrange("p (h d) -> p h d", d=DH)).then_inc(vhi, 1)
                    if hh == 0:
                        if active("MR", t0):
                            i, j = t - OFF["MR"], t0 - OFF["MR"]
                            act.wait_ge(mtr, i + 1)
                            need(act, mdm, 16 * i, 16 * j)
                            act.activation(mrow[:, :], ps_n[0:G * TB, 0:P], ACT.Copy, scale=-1.0 / MAX_SCALE).then_inc(mev, 1)

            steps(act, body, 0, WEIGHTS_AT)
            act.wait_ge(w_in, N_LOADS * 16)
            act.copy(wqk_v[:, :, 0], wraw_qk).then_inc(w_hi, 1)
            act.copy(wv[:, 0], wraw_v).then_inc(w_hi, 1)
            act.copy(wo[:, 0], wraw_o).then_inc(w_hi, 1)
            steps(act, body, WEIGHTS_AT, OFF["PV"])
            act.wait_ge(w_lo, 3)
            act.wait_ge(w_st, 16)
            steps(act, body, OFF["PV"])

        @block.vector
        def _(dve):
            def maxima(t, t0, hh, tiles):
                i, j = t - OFF["SM"], t0 - OFF["SM"]
                if active("SM", t0):
                    for qt in tiles:
                        dve.wait_ge(scq, 16 * i + 4 * hh + qt + 1)
                        need(dve, mtr, i - 1 , j - 1)
                        col = hh * TB + qt
                        dve.tensor_reduce(nmax[:, bass.ds(j % 2, 1), col:col + 1].rearrange("p a c -> p (a c)"),
                                          ps_s[qt % 2][:, :], AX_X, ALU.max).then_inc(smax, 1)

            def remainder(i, hh):
                dve.wait_ge(pexp, 3 * (G * i + hh) + 3)
                p = probs[:, hh % 2, 2:4, :].rearrange("p a s -> p (a s)")
                dve.tensor_tensor(plo[:, hh % 2, 2:4, :].rearrange("p a s -> p (a s)"), p,
                                  p.bitcast(BF16)[:, 1::2], ALU.subtract).then_inc(plo_v, 1)

            def reciprocal(i, j, hh):
                m, m0 = G * i + hh, G * j + hh
                dve.wait_ge(oev, m + 1)
                need(dve, onm, m - 1, m0 - 1)
                dve.reciprocal(o_rec[:, hh % 2, :], o_raw[:, hh % 2, :, 2 * DH]).then_inc(orc, 1)

            def body(t, t0):
                for hh in range(G):
                    if hh == 0:
                        if active("TL", t0):
                            remainder(t - OFF["TL"], G - 1)
                    elif active("PV", t0):
                        remainder(t - OFF["PV"], hh - 1)
                    maxima(t, t0, hh, (0, 1))
                    if hh < 2:
                        if active("TL", t0):
                            reciprocal(t - OFF["TL"], t0 - OFF["TL"], hh + 2)
                    elif active("PV", t0):
                        reciprocal(t - OFF["PV"], t0 - OFF["PV"], hh - 2)
                    if hh == 2 and active("PR", t0) and masked_rows(t0):
                        i, j = t - OFF["PR"], t0 - OFF["PR"]
                        dve.wait_ge(prj, i + 1)
                        need(dve, qhi, i, j)
                        need(dve, qlo, i, j)
                        dve.scalar_tensor_tensor(out=q32[:, :], in0=ps_m[:, :], scalar=bqk[:, bass.ds(j % 4, 1)],
                                                 in1=rowany[:, bass.ds(j % 2, 1), :].rearrange("p a s -> p (a s)"),
                                                 op0=ALU.add, op1=ALU.mult).then_inc(q32d, 1)
                    maxima(t, t0, hh, (2, 3))
                    if hh == 0 and active("OP", t0):
                        i, j = t - OFF["OP"], t0 - OFF["OP"]
                        dve.wait_ge(oprj, i + 1)
                        dve.wait_ge(xb, i + 1)
                        xi = x_sb[:, bass.ds(i, 1), :].rearrange("p a d -> p (a d)")
                        dve.tensor_tensor(xi, ps_m[:, 0:D], xi, ALU.add).then_inc(xout, 1)
                    if hh == 0 and active("LN", t0):
                        i, j = t - OFF["LN"], t0 - OFF["LN"]
                        if layer == 0:
                            dve.wait_ge(x_in, 16 * (i + 1))
                        need(dve, mvd, i, j)
                        dve.bn_stats(stat[:, :], x_sb[:, bass.ds(i, 1), :].rearrange("p a d -> p (a d)")).then_inc(bn, 1)
                        upto = in_register(dve, i + 1)
                        settle(dve, setup_g, G_FIRST)
                        dve.wait_ge(bn, upto)
                        need(dve, rsd, i, j)
                        dve.bn_aggr(mv[:, :], stat[:, :]).then_inc(mvd, 1)
                    if hh == 2 and active("VP", t0):
                        i, j = t - OFF["VP"], t0 - OFF["VP"]
                        dve.wait_ge(vprj, i + 1)
                        need(dve, vlo, i, j)
                        need(dve, vhi, i, j)
                        dve.tensor_tensor(v32[:, :], ps_n[:, 0:D], bv_b[:, :], ALU.add).then_inc(v32d, 1)
                    if hh == 3 and active("OT", t0):
                        i, j = t - OFF["OT"], t0 - OFF["OT"]
                        dve.wait_ge(ohi, i + 1)
                        dve.tensor_tensor(oT[:, 1], ps_m[:, 0:D].rearrange("p (k c) -> p k c", k=KT),
                                          oT[:, 0].bitcast(F32), ALU.subtract).then_inc(olo, 1)
                    if hh == 3 and active("LN", t0):
                        i, j = t - OFF["LN"], t0 - OFF["LN"]
                        dve.wait_ge(xhi, i + 1)
                        at = bass.ds(parity(i) * 8, KT)
                        to = bass.ds(parity(i) * 8 + KT, KT)
                        cols = bass.ds((j % TB) * P, P)
                        dve.tensor_tensor(src[:, to, cols], ps_n[:, 0:D].rearrange("p (k c) -> p k c", k=KT),
                                          src[:, at, cols].bitcast(F32), ALU.subtract).then_inc(xlo, 1)

            if layer == 0:
                q_rows = stack[:, :, :].bitcast(F32).rearrange("p (a k h) s -> p a k (h s)", k=2, h=8)[:, :, 0, :]
                dve.memset(q_rows, 0.0).then_inc(setup_w, 1)
                dve.memset(rowany[:, 1, :], 1.0).then_inc(setup_w, 1)
            steps(dve, body, 0, WEIGHTS_AT)
            if layer == 0:
                dve.wait_ge(w_in, N_LOADS * 16)
                dve.tensor_scalar(keep, mraw, 0.0, None, ALU.not_equal).then_inc(setup_v, 1)
                dve.wait_ge(setup_v, 1)
                dve.tensor_reduce(kept[:, :], keep.rearrange("p a s -> p (a s)"), AX_X, ALU.add).then_inc(setup_v, 1)
                dve.wait_ge(setup_p, 1)
                dve.tensor_scalar(rowany[:, 0, :], ps_m[:, :], 1.0, None, ALU.min).then_inc(setup_v, 1)
                dve.tensor_scalar(maskT[:, :, :], keep, 1.0, MASK_BIG, ALU.subtract, ALU.mult).then_inc(setup_v, 1)
                dve.wait_ge(setup_v, 4)
                for kt in range(TB):
                    dve.tensor_tensor(maskT[:, kt, :], maskT[:, kt, :], rowany[:, 0, :], ALU.mult).then_inc(setup_v, 1)
                dve.wait_ge(setup_p, 2)
                dve.tensor_copy(kept_all[:, :], ps_o[0:1, 0:1]).then_inc(setup_v, 1)
            else:
                dve.memset(rowany[:, :, :].rearrange("p a s -> p (a s)"), 1.0).then_inc(setup_v, 1)
                dve.wait_ge(w_in, N_LOADS * 16)
            dve.wait_ge(setup_v, V_SETUP)
            dve.wait_ge(b_in, N_BIASES * 16)
            dve.wait_ge(w_hi, 1)
            dve.tensor_tensor(wqk_v[:, :, 1], wraw_qk, wqk_v[:, :, 0].bitcast(F32), ALU.subtract).then_inc(w_lo, 1)
            dve.wait_ge(w_hi, 2)
            dve.tensor_tensor(wv[:, 1], wraw_v, wv[:, 0].bitcast(F32), ALU.subtract).then_inc(w_lo, 1)
            dve.wait_ge(w_hi, 3)
            dve.tensor_tensor(wo[:, 1], wraw_o, wo[:, 0].bitcast(F32), ALU.subtract).then_inc(w_lo, 1)
            if layer == 0:
                dve.wait_ge(setup_w, 2)
            steps(dve, body, WEIGHTS_AT)

        @block.gpsimd
        def _(pool):
            pool.memset(half[:, :], -0.5).then_inc(setup_g, 1)
            pool.memset(identb[:, :], 0.0).then_inc(setup_g, 1)
            if layer == 0:
                pool.memset(ident_sb[:, :], 0.0).then_inc(setup_g, 1)
                pool.wait_ge(setup_g, 3)
                pool.affine_select(out=ident_sb[:, :], in_=ident_sb[:, :], compare_op=ALU.not_equal, fill=1.0,
                                   base=0, pattern=[[-1, P]], channel_multiplier=1).then_inc(setup_g, 1)
            pool.wait_ge(setup_g, 2)
            pool.affine_select(out=identb[:, :], in_=identb[:, :], compare_op=ALU.not_equal, fill=1.0,
                               base=0, pattern=[[-1, P]], channel_multiplier=1).then_inc(setup_g, 1)
            pool.wait_ge(setup_g, G_FIRST)
            pool.wait_ge(b_in, N_BIASES * 16)

            def remainder(t, t0, hh):
                i, j = t - OFF["PV"], t0 - OFF["PV"]
                if active("PV", t0):
                    m, m0 = G * i + hh, G * j + hh
                    pool.wait_ge(pexp, 3 * m + 1)
                    p = probs[:, hh % 2, 0:2, :].rearrange("p a s -> p (a s)")
                    pool.tensor_tensor(plo[:, hh % 2, 0:2, :].rearrange("p a s -> p (a s)"), p,
                                       p.bitcast(BF16)[:, 1::2], ALU.subtract).then_inc(plo_g, 1)

            def normalise(i, j, hh):
                m, m0 = G * i + hh, G * j + hh
                pool.wait_ge(oev, m + 1)
                need(pool, onm, m - 1, m0 - 1)
                pool.tensor_tensor(o_sum[:, hh % 2], o_raw[:, hh % 2, :, 0:DH], o_raw[:, hh % 2, :, DH:2 * DH],
                                   ALU.add).then_inc(oad, 1)
                pool.wait_ge(oad, m + 1)
                pool.wait_ge(orc, m + 1)
                need(pool, onow, 16 * prior_batch(i), 16 * prior_batch(j))
                head = (j % 4) * G + hh
                pool.tensor_tensor(o_sb[:, bass.ds(parity(i) * TB, TB), bass.ds(head * DH, DH)], o_sum[:, hh % 2],
                                   o_rec[:, hh % 2, :].unsqueeze(2).to_broadcast([P, TB, DH]), ALU.mult).then_inc(onm, 1)

            def body(t, t0):
                for hh in range(G):
                    remainder(t, t0, hh)
                    if hh < 2:
                        if active("TL", t0):
                            normalise(t - OFF["TL"], t0 - OFF["TL"], hh + 2)
                    elif active("PV", t0):
                        normalise(t - OFF["PV"], t0 - OFF["PV"], hh - 2)
                    i, j = t - OFF["LN"], t0 - OFF["LN"]
                    if hh == 0 and active("LN", t0):
                        pool.wait_ge(chi, i + 1)
                        at = bass.ds(parity(i) * 8 + 4, KT)
                        to = bass.ds(parity(i) * 8 + 4 + KT, KT)
                        cols = bass.ds((j % TB) * P, P)
                        pool.tensor_tensor(src[:, to, cols], craw[:, bass.ds(j % 2, 1)].rearrange("p a k c -> p (a k) c"), src[:, at, cols].bitcast(F32),
                                           ALU.subtract).then_inc(clo, 1)
                    if hh == 1 and active("LN", t0):
                        upto = in_register(pool, i + 1)
                        settle(pool, setup_g, G_FIRST)
                        pool.wait_ge(mvd, upto)
                        need(pool, xnd, i, j)
                        pool.tensor_scalar(rstd[:, 0:1], mv[:, 1:2], EPS, None, ALU.add).then_inc(var1, 1)
                        pool.wait_ge(var1, i + 1)
                        pool.tensor_tensor(rstd[:, 1:2], rstd[:, 0:1], half[:, :], ALU.pow).then_inc(pwd, 1)
                        settle(pool, setup_g, G_FIRST)
                        pool.wait_ge(pwd, upto)
                        pool.tensor_scalar(rstd[:, 2:3], mv[:, 0:1], rstd[:, 1:2], -1.0, ALU.mult, ALU.mult).then_inc(rsd, 1)
                    if hh == 3 and active("LN", t0):
                        pool.wait_ge(xnd, i + 1)
                        xi = x_sb[:, bass.ds(i, 1), :].rearrange("p a d -> p (a d)")
                        pool.tensor_tensor(xi, xi, bo_b[:, :], ALU.add).then_inc(xb, 1)
                    i, j = t - OFF["PR"], t0 - OFF["PR"]
                    if hh == 3 and active("PR", t0):
                        pool.wait_ge(qhi, i + 1)
                        pool.tensor_tensor(qhl[:, 1, :], q32[:, :], qhl[:, 0, :], ALU.subtract).then_inc(qlo, 1)
                    i, j = t - OFF["VP"], t0 - OFF["VP"]
                    if hh == 3 and active("VP", t0):
                        pool.wait_ge(vhi, i + 1)
                        heads = bass.ds(parity(i) * TB * H + (j % TB) * H, H)
                        pool.tensor_tensor(v16[:, heads, DH:2 * DH], v32[:, :].rearrange("p (h d) -> p h d", d=DH),
                                           v16[:, heads, 0:DH], ALU.subtract).then_inc(vlo, 1)

            steps(pool, body, 0, WEIGHTS_AT)
            if layer == 0:
                pool.memset(onesb[:, :], 1.0).then_inc(setup_g, 1)
                pool.memset(onesf[:, :], 1.0).then_inc(setup_g, 1)
                k_rows = stack[:, :, :].bitcast(F32).rearrange("p (a k h) s -> p a k (h s)", k=2, h=8)[:, :, 1, :]
                pool.memset(k_rows, MAX_SCALE_TWICE).then_inc(setup_g, 1)
            pool.memset(v16[:, :, :].rearrange("p a w -> p (a w)"), 1.0).then_inc(setup_g, 1)
            pool.wait_ge(setup_g, G_SETUP)
            steps(pool, body, WEIGHTS_AT)


def ffn_phase(nc, layer, x_sb, ident_sb, ins, out, B, S, D, FF):
    TB = S // P
    KT = D // P
    NC = FF // P
    NB = 16
    TOPK = NB // 4
    ROUNDS = TB // 2
    OFF = dict(LN=0, MM=1, YT=2)
    RANGES = [(t, t + 1) for t in range(3)] + ([(3, B)] if B > 3 else [])
    RANGES += [(t, t + 1) for t in range(max(B, 3), B + 2)]

    def active(name, t0):
        return OFF[name] <= t0 < OFF[name] + B

    with ExitStack() as ctx:
        ctx.enter_context(nc.cleanup_on_exit())

        def sb(name, shape, dt):
            return ctx.enter_context(nc.sbuf_tensor(f"L{layer}f_{name}", shape, dt))

        def pb(name, shape, dt):
            return ctx.enter_context(nc.psum_tensor(f"L{layer}f_{name}", shape, dt))

        def sem(name):
            return nc.alloc_semaphore(name=f"L{layer}f_{name}")

        w1 = sb("w1", [P, 2, KT, FF], FR)
        w2 = sb("w2", [P, 2, NC, D], FR)
        w1raw = sb("w1raw", [P, KT, FF], F32)
        w2raw = sb("w2raw", [P, NC, D], F32)
        b1 = sb("b1", [P, NC], F32)
        b2_b = sb("b2_b", [P, 1, D], F32)
        stat = sb("stat", [P, TB, 6], F32)
        mv = sb("mv", [P, TB, 2], F32)
        rstd = sb("rstd", [P, 2, TB], F32)
        half = sb("half", [P, TB], F32)
        xn = sb("xn", [P, TB, D], F32)
        xnT = sb("xnT", [P, 2 * 2 * KT, S], FR)
        h32 = sb("h32", [P, 2, S], F32)
        hT = sb("hT", [P, 2, 2, S], FR)
        if layer == 0:
            rwraw = sb("rwraw", [P, KT, NB], F32)
            rw = sb("rw", [P, 2, KT, NB], FR)
            rb = sb("rb", [NB, 1], F32)
            lgT = sb("lgT", [NB, S], F32)
            lg = sb("lg", [P, TB, NB], F32)
            top8 = sb("top8", [P, TB, 8], F32)
            marked = sb("marked", [P, TB, NB], F32)
            pen = sb("pen", [P, TB, NB], BF16)
            penT = sb("penT", [P, 2, S], BF16)
            spread = sb("spread", [P, FF], BF16)
            identb = sb("identb", [P, P], BF16)

        ps_h = [pb(f"ps_h{c}", [P, S], F32) for c in range(2)]
        ps_y = [pb(f"ps_y{c}", [P, 2, D], F32) for c in range(ROUNDS)]
        ps_x = [pb(f"ps_x{c}", [P, 2, KT, P], F32) for c in range(ROUNDS)]
        if layer == 0:
            ps_r = pb("ps_r", [P, S], F32)
            ps_q = pb("ps_q", [P, 512], F32)
            ps_pen = ps_r[:, :].bitcast(BF16)

        w_in, w_hi, w_lo, const = sem("w_in"), sem("w_hi"), sem("w_lo"), sem("const")
        bn, mvd, var1, rsd, xnd = sem("bn"), sem("mvd"), sem("var1"), sem("rsd"), sem("xnd")
        xt, xhi, xlo, xb = sem("xt"), sem("xhi"), sem("xlo"), sem("xb")
        lgp, lge, lgt, lgc = sem("lgp"), sem("lge"), sem("lgt"), sem("lgc")
        top, abs8, mrk, pnd, pnt, pne = sem("top"), sem("abs8"), sem("mrk"), sem("pnd"), sem("pnt"), sem("pne")
        hp, h32d, hhi, hlo = sem("hp"), sem("h32d"), sem("hhi"), sem("hlo")
        yp, yout = sem("yp"), sem("yout")
        stored = sem("stored")
        N_LOADS = 6 if layer == 0 else 4
        N_SPLITS = 3 if layer == 0 else 2
        N_CONST = 7 if layer == 0 else 1

        def steps(eng, body):
            for t0, t1 in RANGES:
                if t1 - t0 == 1:
                    body(t0, t0)
                else:
                    with eng.Fori(t0, t1) as t:
                        body(t, t0)

        def parity(i):
            return i % 2

        block = ctx.enter_context(nc.Block())

        @block.sync
        def _(sp):
            sp.dma_start(w1raw[:, :, :], ins["w1"].rearrange("(k p) c -> p k c", p=P)).then_inc(w_in, 16)
            sp.dma_start(w2raw[:, :, :], ins["w2"].rearrange("(k p) c -> p k c", p=P)).then_inc(w_in, 16)
            sp.dma_start(b1[:, :], ins["b1"].rearrange("(m p) -> p m", p=P),
                         allow_slow_non_contiguous=True).then_inc(w_in, 16)
            sp.dma_start(b2_b[:, 0, :], ins["b2"].partition_broadcast(P)).then_inc(w_in, 16)
            if layer == 0:
                sp.dma_start(rwraw[:, :, :], ins["rw"].rearrange("(k p) c -> p k c", p=P)).then_inc(w_in, 16)
                sp.dma_start(rb[:, :], ins["rb"].rearrange("(p o) -> p o", o=1)).then_inc(w_in, 16)

            def body(t, t0):
                if out is not None and active("YT", t0):
                    i = t - OFF["YT"]
                    sp.wait_ge(yout, ROUNDS * (i + 1))
                    sp.dma_start(out[:, bass.ds(i * TB, TB), :], x_sb[:, bass.ds(i * TB, TB), :]).then_inc(stored, 16)

            if out is not None:
                steps(sp, body)
                sp.wait_ge(stored, 16 * B)

        @block.tensor
        def _(pe):
            def split3(out_ap, lhs, rhs, n, more=False, **flags):
                pairs = [(a, b, k) for a, b in ((0, 0), (0, 1), (1, 0)) for k in range(n)]
                for m, (a, b, k) in enumerate(pairs):
                    last = pe.matmul(out_ap, lhs(a, k), rhs(b, k), start=(m == 0), stop=(m == len(pairs) - 1 and not more))
                return last

            def turned(i, b, k):
                return xnT[:, bass.ds(parity(i) * 2 * KT + b * KT + k, 1), :].rearrange("p a s -> p (a s)")

            def first_product(i, j, c):
                n, n0 = NC * i + c, NC * j + c
                if c == 0:
                    pe.wait_ge(xhi, ROUNDS * (i + 1))
                    pe.wait_ge(xlo, ROUNDS * (i + 1))
                    if layer == 0:
                        pe.wait_ge(pne, i + 1)
                need(pe, h32d, n - 1, n0 - 1)
                last = split3(ps_h[c % 2][:, :], lambda a, k: w1[:, a, k, c * P:(c + 1) * P],
                              lambda b, k: turned(i, b, k), KT, more=(layer == 0))
                if layer == 0:
                    last = pe.matmul(ps_h[c % 2][:, :], spread[:, c * P:(c + 1) * P],
                                     penT[:, bass.ds(parity(i), 1), :].rearrange("p a s -> p (a s)"), start=False, stop=True)
                last.then_inc(hp, 1)

            def second_product(i, j, c):
                n = NC * i + c
                pe.wait_ge(hhi, n + 1)
                pe.wait_ge(hlo, n + 1)
                if c == 0:
                    need(pe, yout, ROUNDS * i, ROUNDS * j)
                for tt in range(TB):
                    for m, (a, b) in enumerate(((0, 0), (0, 1), (1, 0))):
                        last = pe.matmul(ps_y[tt // 2][:, tt % 2, :], hT[:, c % 2, a, tt * P:(tt + 1) * P], w2[:, b, c, :],
                                         start=(c == 0 and m == 0 and tt % 2 == 0), stop=(c == NC - 1 and m == 2 and tt % 2 == 1),
                                         skip_group_check=True)
                last.then_inc(yp, 1)

            def turn_x(i, j, r):
                pe.wait_ge(xnd, TB * i + 2 * r + 2)
                need(pe, xhi, ROUNDS * (i - 1) + r + 1, ROUNDS * (j - 1) + r + 1)
                need(pe, xlo, ROUNDS * (i - 1) + r + 1, ROUNDS * (j - 1) + r + 1)
                for tt in range(2):
                    for k in range(KT):
                        last = pe.transpose(ps_x[r][:, tt, k, :], xn[:, 2 * r + tt, k * P:(k + 1) * P], ident_sb[:, :])
                last.then_inc(xt, 1)

            def logits(i, j):
                pe.wait_ge(xhi, ROUNDS * (i + 1))
                pe.wait_ge(xlo, ROUNDS * (i + 1))
                need(pe, pne, i, j)
                split3(ps_r[0:NB, :], lambda a, k: rw[:, a, k, :], lambda b, k: turned(i, b, k), KT).then_inc(lgp, 1)

            def turn_logits(i, j):
                settle(pe, const, N_CONST)
                pe.wait_ge(lge, i + 1)
                need(pe, lgc, i, j)
                for tt in range(TB):
                    last = pe.transpose(ps_q[:, tt * NB:(tt + 1) * NB], lgT[:, tt * P:(tt + 1) * P], ident_sb[0:NB, 0:NB])
                last.then_inc(lgt, 1)

            def turn_penalties(i, j):
                pe.wait_ge(pnd, i + 1)
                for tt in range(TB):
                    last = pe.transpose(ps_pen[0:NB, tt * P:(tt + 1) * P], pen[:, tt, :], identb[:, :])
                last.then_inc(pnt, 1)

            pe.wait_ge(const, 1)

            def body(t, t0):
                i, j = t - OFF["MM"], t0 - OFF["MM"]
                l, l0 = t - OFF["LN"], t0 - OFF["LN"]
                if t0 == OFF["MM"]:
                    pe.wait_ge(w_hi, N_SPLITS)
                    pe.wait_ge(w_lo, N_SPLITS)
                for c in range(NC):
                    if active("MM", t0):
                        first_product(i, j, c)
                    if c == 0:
                        if active("YT", t0):
                            second_product(t - OFF["YT"], t0 - OFF["YT"], NC - 1)
                    elif active("MM", t0):
                        second_product(i, j, c - 1)
                    if active("LN", t0):
                        if c == 2:
                            turn_x(l, l0, 0)
                        if c == 3:
                            turn_x(l, l0, 1)
                        if t0 == 0 and c == 5:
                            pe.wait_ge(const, N_CONST)
                            pe.wait_ge(w_hi, 1)
                            pe.wait_ge(w_lo, 1)
                        if layer == 0 and c == 5:
                            logits(l, l0)
                        if layer == 0 and c == 6:
                            turn_logits(l, l0)
                        if layer == 0 and c == 7:
                            turn_penalties(l, l0)

            steps(pe, body)

        @block.scalar
        def _(act):
            def high_halves():
                act.wait_ge(w_in, 16 * N_LOADS)
                if layer == 0:
                    act.copy(rw[:, 0], rwraw[:, :, :]).then_inc(w_hi, 1)
                act.copy(w1[:, 0], w1raw[:, :, :]).then_inc(w_hi, 1)
                act.copy(w2[:, 0], w2raw[:, :, :]).then_inc(w_hi, 1)

            def body(t, t0):
                i, j = t - OFF["MM"], t0 - OFF["MM"]
                l, l0 = t - OFF["LN"], t0 - OFF["LN"]
                for c in range(NC):
                    if t0 == 0 and c == 5:
                        high_halves()
                    if active("MM", t0):
                        n, n0 = NC * i + c, NC * j + c
                        act.wait_ge(hp, n + 1)
                        need(act, hlo, n - 1, n0 - 1)
                        act.activation(h32[:, c % 2, :], ps_h[c % 2][:, :], ACT.Relu if layer == 0 else ACT.Gelu,
                                       bias=b1[:, c:c + 1]).then_inc(h32d, 1)
                        act.wait_ge(h32d, n + 1)
                        need(act, yp, n - 1, n0 - 1)
                        act.copy(hT[:, c % 2, 0, :], h32[:, c % 2, :]).then_inc(hhi, 1)
                    if active("LN", t0) and c in (3, 4):
                        r = c - 3
                        act.wait_ge(xt, ROUNDS * l + r + 1)
                        need(act, hp, NC * (l - 1), NC * (l0 - 1))
                        act.copy(xnT[:, bass.ds(parity(l) * 2 * KT, KT), 2 * r * P:(2 * r + 2) * P].rearrange("p k (t c) -> p t k c", t=2),
                                 ps_x[r][:, :, :, :]).then_inc(xhi, 1)
                    if active("LN", t0) and layer == 0 and c == 5:
                        act.wait_ge(lgp, l + 1)
                        need(act, lgt, l, l0)
                        act.activation(lgT[:, :], ps_r[0:NB, :], ACT.Identity, bias=rb[:, 0:1]).then_inc(lge, 1)
                    if active("LN", t0) and layer == 0 and c == 7:
                        act.wait_ge(pnt, l + 1)
                        act.copy(penT[0:NB, bass.ds(parity(l), 1), :].rearrange("p a s -> p (a s)"),
                                 ps_pen[0:NB, 0:S]).then_inc(pne, 1)

            steps(act, body)

        @block.vector
        def _(dve):
            def low_halves():
                dve.wait_ge(w_in, 16 * N_LOADS)
                if layer == 0:
                    dve.wait_ge(w_hi, 1)
                    dve.tensor_tensor(rw[:, 1], rwraw[:, :, :], rw[:, 0].bitcast(F32), ALU.subtract).then_inc(w_lo, 1)
                dve.wait_ge(w_hi, N_SPLITS - 1)
                dve.tensor_tensor(w1[:, 1], w1raw[:, :, :], w1[:, 0].bitcast(F32), ALU.subtract).then_inc(w_lo, 1)
                dve.wait_ge(w_hi, N_SPLITS)
                dve.tensor_tensor(w2[:, 1], w2raw[:, :, :], w2[:, 0].bitcast(F32), ALU.subtract).then_inc(w_lo, 1)

            def body(t, t0):
                i, j = t - OFF["MM"], t0 - OFF["MM"]
                l, l0 = t - OFF["LN"], t0 - OFF["LN"]
                for c in range(NC):
                    if t0 == 0 and c == 5:
                        low_halves()
                    if c == 0 and active("LN", t0):
                        for tt in range(TB):
                            need(dve, mvd, TB * l, TB * l0)
                            dve.bn_stats(stat[:, tt, :], x_sb[:, bass.ds(TB * l + tt, 1), :].rearrange("p a d -> p (a d)")).then_inc(bn, 1)
                        upto = in_register(dve, TB * (l + 1))
                        settle(dve, const, 1)
                        dve.wait_ge(bn, upto)
                        need(dve, xnd, TB * l, TB * l0)
                        need(dve, rsd, l, l0)
                        for tt in range(TB):
                            dve.bn_aggr(mv[:, tt, :], stat[:, tt, :]).then_inc(mvd, 1)
                    if c == 1:
                        if active("YT", t0):
                            y = t - OFF["YT"]
                            dve.wait_ge(yp, NC * (y + 1))
                            dve.wait_ge(xb, y + 1)
                            for r in range(ROUNDS):
                                xi = x_sb[:, bass.ds(TB * y + 2 * r, 2), :]
                                dve.tensor_tensor(xi, ps_y[r][:, :, :], xi, ALU.add).then_inc(yout, 1)
                        if active("LN", t0):
                            dve.wait_ge(rsd, l + 1)
                            need(dve, xt, ROUNDS * l, ROUNDS * l0)
                            for tt in range(TB):
                                dve.tensor_scalar(xn[:, tt, :], x_sb[:, bass.ds(TB * l + tt, 1), :].rearrange("p a d -> p (a d)"),
                                                  mv[:, tt, 0:1], rstd[:, 1, tt:tt + 1], ALU.subtract, ALU.mult).then_inc(xnd, 1)
                    if active("MM", t0):
                        n, n0 = NC * i + c, NC * j + c
                        dve.wait_ge(hhi, n + 1)
                        dve.tensor_tensor(hT[:, c % 2, 1, :], h32[:, c % 2, :], hT[:, c % 2, 0, :].bitcast(F32), ALU.subtract).then_inc(hlo, 1)
                    if active("LN", t0) and c in (3, 4):
                        r = c - 3
                        dve.wait_ge(xhi, ROUNDS * l + r + 1)
                        cols = slice(2 * r * P, (2 * r + 2) * P)
                        hi = xnT[:, bass.ds(parity(l) * 2 * KT, KT), cols]
                        lo = xnT[:, bass.ds(parity(l) * 2 * KT + KT, KT), cols]
                        for tt in range(2):
                            at = slice(tt * P, (tt + 1) * P)
                            ins_ = dve.tensor_tensor(lo[:, :, at], ps_x[r][:, tt, :, :], hi[:, :, at].bitcast(F32), ALU.subtract)
                        ins_.then_inc(xlo, 1)
                    if active("LN", t0) and layer == 0 and c == 6:
                        dve.wait_ge(lgt, l + 1)
                        need(dve, mrk, TB * l, TB * l0)
                        dve.tensor_copy(lg[:, :, :].rearrange("p t b -> p (t b)"), ps_q[:, 0:TB * NB]).then_inc(lgc, 1)
                        settle(dve, const, 1)
                        dve.wait_ge(lgc, l + 1)
                        for tt in range(TB):
                            dve.max(top8[:, tt, :], lg[:, tt, :]).then_inc(top, 1)
                        dve.wait_ge(top, TB * (l + 1))
                        dve.memset(top8[:, :, TOPK:8], -3.0e38).then_inc(abs8, 1)
                        settle(dve, const, 1)
                        dve.wait_ge(abs8, l + 1)
                        need(dve, pnd, l, l0)
                        for tt in range(TB):
                            dve.match_replace(marked[:, tt, :], top8[:, tt, :], lg[:, tt, :], 3.0e38).then_inc(mrk, 1)
                        dve.wait_ge(mrk, TB * (l + 1))
                        need(dve, pnt, l, l0)
                        dve.tensor_scalar(pen[:, :, :], marked[:, :, :], 3.0e38, -BLOCK_BIG, ALU.is_lt, ALU.mult).then_inc(pnd, 1)

            steps(dve, body)

        @block.gpsimd
        def _(pool):
            pool.memset(half[:, :], -0.5).then_inc(const, 1)
            pool.wait_ge(const, 1)

            def constants():
                pool.memset(identb[:, :], 0.0).then_inc(const, 1)
                pool.memset(spread[:, :], 1.0).then_inc(const, 1)
                pool.memset(penT[:, :, :].rearrange("p a s -> p (a s)"), 0.0).then_inc(const, 1)
                pool.wait_ge(const, 3)
                pool.affine_select(out=identb[:, :], in_=identb[:, :], compare_op=ALU.not_equal, fill=1.0,
                                   base=0, pattern=[[-1, P]], channel_multiplier=1).then_inc(const, 1)
                width = FF // NB
                pool.affine_select(out=spread[:, :], in_=spread[:, :], compare_op=ALU.is_ge, fill=0.0,
                                   base=0, pattern=[[1, FF]], channel_multiplier=-width).then_inc(const, 1)
                pool.wait_ge(const, 6)
                pool.affine_select(out=spread[:, :], in_=spread[:, :], compare_op=ALU.is_ge, fill=0.0,
                                   base=width - 1, pattern=[[-1, FF]], channel_multiplier=width).then_inc(const, 1)

            def body(t, t0):
                l, l0 = t - OFF["LN"], t0 - OFF["LN"]
                if active("LN", t0):
                    upto, before = in_register(pool, TB * (l + 1)), in_register(pool, TB * l)
                    settle(pool, const, 1)
                    pool.wait_ge(mvd, upto)
                    need(pool, xnd, before, TB * l0)
                    pool.tensor_scalar(rstd[:, 0, :], mv[:, :, 1], EPS, None, ALU.add).then_inc(var1, 1)
                    pool.wait_ge(var1, l + 1)
                    pool.tensor_tensor(rstd[:, 1, :], rstd[:, 0, :], half[:, :], ALU.pow).then_inc(rsd, 1)
                    if t0 == 0 and layer == 0:
                        constants()
                    if t0 == 0:
                        pool.wait_ge(w_in, 16 * N_LOADS)
                    pool.wait_ge(xnd, TB * (l + 1))
                    xi = x_sb[:, bass.ds(TB * l, TB), :]
                    pool.tensor_tensor(xi, xi, b2_b[:, :, :].to_broadcast([P, TB, D]), ALU.add).then_inc(xb, 1)

            steps(pool, body)


def build(nc, x, ctxT, maskT, wq0, bq0, wk0, bk0, wv0, bv0, wo0, bo0, rw, rb, w1a, b1a, w2a, b2a,
          wq1, bq1, wk1, bk1, wv1, bv1, wo1, bo1, w1b, b1b, w2b, b2b, out):
    B, S, D = x.shape
    NT = B * S // P
    scratch = nc.dram_tensor("scratch", (2, 2, P, S), F16).ap()
    scratch_w = nc.dram_tensor("scratch_w", (4, P, 4 * P), F32).ap()
    with ExitStack() as ctx:
        x_sb = ctx.enter_context(nc.sbuf_tensor("x_sb", [P, NT, D], F32))
        ident_sb = ctx.enter_context(nc.sbuf_tensor("ident_sb", [P, P], F32))
        stack = ctx.enter_context(nc.sbuf_tensor("stack", [P, 2 * 4 * 8, S], F16))
        xt = x.rearrange("b (t p) d -> p (b t) d", p=P)
        outt = out.rearrange("b (t p) d -> p (b t) d", p=P)
        attention_phase(nc, 0, x_sb, ident_sb, stack,
                        dict(x=xt, ctxT=ctxT, maskT=maskT, wqT=wq0, bq=bq0, wkT=wk0, bk=bk0, wvT=wv0, bv=bv0, woT=wo0, bo=bo0),
                        scratch, scratch_w, B, S, D)
        ffn_phase(nc, 0, x_sb, ident_sb, dict(rw=rw, rb=rb, w1=w1a, b1=b1a, w2=w2a, b2=b2a), None, B, S, D, w1a.shape[1])
        attention_phase(nc, 1, x_sb, ident_sb, stack,
                        dict(ctxT=ctxT, wqT=wq1, bq=bq1, wkT=wk1, bk=bk1, wvT=wv1, bv=bv1, woT=wo1, bo=bo1),
                        scratch, scratch_w, B, S, D)
        ffn_phase(nc, 1, x_sb, ident_sb, dict(w1=w1b, b1=b1b, w2=w2b, b2=b2b), outt, B, S, D, w1b.shape[1])


_LAYOUT = [
    ("x", None), ("ctx_1024", "tokens"), ("mask_1x1xSxS2_if1", "mask"),
    ("L0_xattn_w_Q", "T"), ("L0_xattn_b_Q", None), ("L0_xattn_w_K", "T"), ("L0_xattn_b_K", None),
    ("L0_xattn_w_V", "T"), ("L0_xattn_b_V", None), ("L0_xattn_w_O", "T"), ("L0_xattn_b_O", None),
    ("L0_ffn_router_w", "T"), ("L0_ffn_router_b", None), ("L0_ffn_w1", "T"), ("L0_ffn_b1", None),
    ("L0_ffn_w2", "T"), ("L0_ffn_b2", None),
    ("L1_xattn_wq_w", "T"), ("L1_xattn_wq_b", None), ("L1_xattn_wk_w", "T"), ("L1_xattn_wk_b", None),
    ("L1_xattn_wv_w", "T"), ("L1_xattn_wv_b", None), ("L1_xattn_wo_w", "T"), ("L1_xattn_wo_b", None),
    ("L1_ffn_w1", None), ("L1_ffn_b1", None), ("L1_ffn_w2", None), ("L1_ffn_b2", None),
]


def kernel(**inputs):
    import numpy as _np
    import concourse.bacc as _bacc
    from concourse import mybir as _mybir
    from concourse.bass_utils import run_bass_kernel_spmd as _run

    nc = _bacc.Bacc("TRN2", target_bir_lowering=False, num_devices=1)
    arrays, args = {}, []
    for name, how in _LAYOUT:
        a = _np.asarray(inputs[name])
        if how == "tokens":
            a = a.reshape(-1, a.shape[-1])
        if how == "mask":
            a = a.reshape(a.shape[-2], a.shape[-1])
        if how is not None:
            a = a.T
        a = _np.ascontiguousarray(a)
        arrays[f"in_{name}"] = a
        args.append(nc.dram_tensor(f"in_{name}", a.shape, _mybir.dt.from_np(a.dtype), kind="ExternalInput").ap())
    shape = inputs["x"].shape
    args.append(nc.dram_tensor("out_0", shape, _mybir.dt.float32, kind="ExternalOutput").ap())
    build(nc, *args)
    r = _run(nc, [arrays], core_ids=[0])
    return r.results[0]["out_0"]
```
